# Optimizing a Trainium2 kernel written in Bass

```python
import numpy as np
import jax
import jax.numpy as jnp

def _softmax(x, axis=-1):
    return jax.nn.softmax(x, axis=axis)

def _gelu(x):
    return jax.nn.gelu(x, approximate=True)

def _silu(x):
    return jax.nn.silu(x)

def _sigmoid(x):
    return jax.nn.sigmoid(x)

def _layernorm(x, axis=-1, eps=1e-05):
    m = jnp.mean(x, axis=axis, keepdims=True)
    v = jnp.var(x, axis=axis, keepdims=True)
    return (x - m) / jnp.sqrt(v + eps)

def _scatter_add(tgt, idx, src, axis=0):
    return tgt.at[idx].add(src)

def _segment_sum(src, seg, n):
    return jax.ops.segment_sum(src, seg, n)
kernel_name = 'mk_cond_resid_d4_seqx_r4_f90f0a'

def setup_inputs(seed: int=0):
    np.random.seed(seed)
    _w = jnp.asarray

    def _rec_inputs():
        import jax
        import jax.numpy as jnp
        _rk = jax.random.key(seed)
        x = 7.22e-05 + 1 * jax.random.normal(jax.random.fold_in(_rk, 1), (4, 512, 256), jnp.float32)
        _lenS = 512 - jax.random.randint(jax.random.fold_in(_rk, 7), (4,), 0, max(1, 512 // 4) + 1, jnp.int32)
        _lenS2 = 512 - jax.random.randint(jax.random.fold_in(_rk, 8), (4,), 0, max(1, 512 // 4) + 1, jnp.int32)
        cond_8 = jax.random.uniform(jax.random.fold_in(_rk, 11), (4, 8), jnp.float32, 0.0, 0.999837)
        return (x, cond_8)
    x, cond_8 = _rec_inputs()

    def _L0_cond_setup():
        import jax, jax.numpy as jnp
        import numpy as np
        key = jax.random.key(seed)
        k1, k2, k3, k4, k5 = jax.random.split(key, 5)
        B, N, T, O, G = (32, 64, 256, 256, 8)
        x = jax.random.normal(k1, (B, N, T), dtype=jnp.float32)
        y = jax.random.uniform(k2, (B, G), dtype=jnp.float32)
        weight = jax.random.normal(k3, (G, O, T), dtype=jnp.float32) * (1.0 / np.sqrt(T))
        mask = jax.random.uniform(k4, (O, T), dtype=jnp.float32)
        bias = jax.random.normal(k5, (O,), dtype=jnp.float32)
        return {'x': x, 'y': y, 'weight': weight, 'mask': mask, 'bias': bias}
    _L0_cond_all = _L0_cond_setup()
    _L0_cond_in = {k: v for k, v in _L0_cond_all.items() if k in ('weight', 'mask', 'bias')}
    del _L0_cond_all

    def _L1_cond_setup():
        import jax, jax.numpy as jnp
        import numpy as np
        R = 16
        ALPHA = 32.0
        SCALING = ALPHA / R
        key = jax.random.key(seed)
        ks = jax.random.split(key, 6)
        B, T, C, O, E = (16, 375, 256, 256, 8)
        x = jax.random.normal(ks[0], (B, T, C), dtype=jnp.float32)
        w = jax.random.uniform(ks[1], (B, E), dtype=jnp.float32)
        W_base = jax.random.normal(ks[2], (O, C), dtype=jnp.float32) * 0.02
        b_base = jax.random.normal(ks[3], (O,), dtype=jnp.float32) * 0.02
        As = jax.random.normal(ks[4], (E, R, C), dtype=jnp.float32) * 0.02
        Bs = jax.random.normal(ks[5], (E, O, R), dtype=jnp.float32) * 0.02
        return {'x': x, 'w': w, 'W_base': W_base, 'b_base': b_base, 'As': As, 'Bs': Bs}
    _L1_cond_all = _L1_cond_setup()
    _L1_cond_in = {k: v for k, v in _L1_cond_all.items() if k in ('W_base', 'b_base', 'As', 'Bs')}
    del _L1_cond_all

    def _L2_cond_setup():
        import jax, jax.numpy as jnp
        import numpy as np
        B, S, D = (16, 512, 256)
        E, H = (8, 512)
        key = jax.random.key(seed)
        ks = jax.random.split(key, 8)
        scale = 0.02
        x = jax.random.normal(ks[0], (B, S, D), dtype=jnp.float32)
        opcode_onehot = jax.random.uniform(ks[1], (B, E), dtype=jnp.float32)
        W_up = jax.random.normal(ks[2], (E, H, D), dtype=jnp.float32) * scale
        b_up = jnp.zeros((E, H), dtype=jnp.float32)
        W_gate = jax.random.normal(ks[3], (E, H, D), dtype=jnp.float32) * scale
        b_gate = jnp.zeros((E, H), dtype=jnp.float32)
        W_down = jax.random.normal(ks[4], (E, D, H), dtype=jnp.float32) * scale
        b_down = jnp.zeros((E, D), dtype=jnp.float32)
        return {'x': x, 'opcode_onehot': opcode_onehot, 'W_up': W_up, 'b_up': b_up, 'W_gate': W_gate, 'b_gate': b_gate, 'W_down': W_down, 'b_down': b_down}
    _L2_cond_all = _L2_cond_setup()
    _L2_cond_in = {k: v for k, v in _L2_cond_all.items() if k in ('W_up', 'b_up', 'W_gate', 'b_gate', 'W_down', 'b_down')}
    del _L2_cond_all

    def _L3_cond_setup():
        import jax, jax.numpy as jnp
        import numpy as np
        TOP_K = 2
        NUM_MOE_LAYERS = 12

        def _gemma_mlp(x, gate_w, up_w, down_w):
            g = jnp.einsum('bsh,hi->bsi', x, gate_w)
            u = jnp.einsum('bsh,hi->bsi', x, up_w)
            return jnp.einsum('bsi,ih->bsh', jax.nn.gelu(g, approximate=True) * u, down_w)
        key = jax.random.key(seed)
        ks = jax.random.split(key, 8)
        B, S, H, I, E = (32, 64, 256, 1024, 8)
        std = 0.02
        return {'x': jax.random.normal(ks[0], (B, S, H), jnp.float32), 'router_logits': jax.random.normal(ks[1], (B, E), jnp.float32), 'skill_gate': jax.random.normal(ks[2], (E, H, I), jnp.float32) * std, 'skill_up': jax.random.normal(ks[3], (E, H, I), jnp.float32) * std, 'skill_down': jax.random.normal(ks[4], (E, I, H), jnp.float32) * std, 'shared_gate': jax.random.normal(ks[5], (H, I), jnp.float32) * std, 'shared_up': jax.random.normal(ks[6], (H, I), jnp.float32) * std, 'shared_down': jax.random.normal(ks[7], (I, H), jnp.float32) * std}
    _L3_cond_all = _L3_cond_setup()
    _L3_cond_in = {k: v for k, v in _L3_cond_all.items() if k in ('skill_gate', 'skill_up', 'skill_down', 'shared_gate', 'shared_up', 'shared_down')}
    del _L3_cond_all
    return {'x': x, 'cond_8': cond_8, 'L0_cond_weight': _L0_cond_in['weight'], 'L0_cond_mask': _L0_cond_in['mask'], 'L0_cond_bias': _L0_cond_in['bias'], 'L1_cond_W_base': _L1_cond_in['W_base'], 'L1_cond_b_base': _L1_cond_in['b_base'], 'L1_cond_As': _L1_cond_in['As'], 'L1_cond_Bs': _L1_cond_in['Bs'], 'L2_cond_W_up': _L2_cond_in['W_up'], 'L2_cond_b_up': _L2_cond_in['b_up'], 'L2_cond_W_gate': _L2_cond_in['W_gate'], 'L2_cond_b_gate': _L2_cond_in['b_gate'], 'L2_cond_W_down': _L2_cond_in['W_down'], 'L2_cond_b_down': _L2_cond_in['b_down'], 'L3_cond_skill_gate': _L3_cond_in['skill_gate'], 'L3_cond_skill_up': _L3_cond_in['skill_up'], 'L3_cond_skill_down': _L3_cond_in['skill_down'], 'L3_cond_shared_gate': _L3_cond_in['shared_gate'], 'L3_cond_shared_up': _L3_cond_in['shared_up'], 'L3_cond_shared_down': _L3_cond_in['shared_down']}

def reference(x, cond_8, L0_cond_weight, L0_cond_mask, L0_cond_bias, L1_cond_W_base, L1_cond_b_base, L1_cond_As, L1_cond_Bs, L2_cond_W_up, L2_cond_b_up, L2_cond_W_gate, L2_cond_b_gate, L2_cond_W_down, L2_cond_b_down, L3_cond_skill_gate, L3_cond_skill_up, L3_cond_skill_down, L3_cond_shared_gate, L3_cond_shared_up, L3_cond_shared_down):
    import jax
    import jax.numpy as jnp

    def _L0_cond_ref(x, y, weight, mask, bias):
        import jax, jax.numpy as jnp
        import numpy as np
        masked_w = weight * mask[None, :, :]
        w_bot = jnp.einsum('bg,got->bot', y, masked_w)
        return jnp.einsum('bnt,bot->bno', x, w_bot) + bias

    def _L1_cond_ref(x, w, W_base, b_base, As, Bs):
        import jax, jax.numpy as jnp
        import numpy as np
        R = 16
        ALPHA = 32.0
        SCALING = ALPHA / R
        out = jnp.einsum('btc,oc->bto', x, W_base) + b_base
        h = jnp.einsum('btc,erc->bter', x, As)
        lora = jnp.einsum('bter,eor,be->bto', h, Bs, w)
        return out + lora * SCALING

    def _L2_cond_ref(x, opcode_onehot, W_up, b_up, W_gate, b_gate, W_down, b_down):
        import jax, jax.numpy as jnp
        import numpy as np
        B, S, D = (16, 512, 256)
        E, H = (8, 512)
        expert = jnp.argmax(opcode_onehot, axis=-1)
        wu, bu = (W_up[expert], b_up[expert])
        wg, bg = (W_gate[expert], b_gate[expert])
        wd, bd = (W_down[expert], b_down[expert])
        up = jnp.einsum('bsd,bhd->bsh', x, wu) + bu[:, None, :]
        gate = jnp.einsum('bsd,bhd->bsh', x, wg) + bg[:, None, :]
        hidden = jax.nn.silu(up) * gate
        out = jnp.einsum('bsh,bdh->bsd', hidden, wd) + bd[:, None, :]
        return out

    def _L3_cond_ref(x, router_logits, skill_gate, skill_up, skill_down, shared_gate, shared_up, shared_down):
        import jax, jax.numpy as jnp
        import numpy as np
        TOP_K = 2
        NUM_MOE_LAYERS = 12

        def _gemma_mlp(x, gate_w, up_w, down_w):
            g = jnp.einsum('bsh,hi->bsi', x, gate_w)
            u = jnp.einsum('bsh,hi->bsi', x, up_w)
            return jnp.einsum('bsi,ih->bsh', jax.nn.gelu(g, approximate=True) * u, down_w)
        B = x.shape[0]
        E = skill_gate.shape[0]
        rw = jax.nn.softmax(router_logits.astype(jnp.float32), axis=-1)
        w, sel = jax.lax.top_k(rw, TOP_K)
        w = w / w.sum(axis=-1, keepdims=True)
        w = w.astype(x.dtype)
        scale = 1.0 / NUM_MOE_LAYERS
        w = scale * w + (1.0 - scale) * jax.lax.stop_gradient(w)
        dense_w = jnp.zeros((B, E), x.dtype).at[jnp.arange(B)[:, None], sel].add(w)

        def step(acc, params):
            g, u, d, we = params
            return (acc + we[:, None, None] * _gemma_mlp(x, g, u, d), None)
        out, _ = jax.lax.scan(step, jnp.zeros_like(x), (skill_gate, skill_up, skill_down, dense_w.T))
        out = out + _gemma_mlp(x, shared_gate, shared_up, shared_down)
        return out
    x = x + _L0_cond_ref(x, cond_8, L0_cond_weight, L0_cond_mask, L0_cond_bias)
    x = x + _L1_cond_ref(x, cond_8, L1_cond_W_base, L1_cond_b_base, L1_cond_As, L1_cond_Bs)
    x = x + _L2_cond_ref(x, cond_8, L2_cond_W_up, L2_cond_b_up, L2_cond_W_gate, L2_cond_b_gate, L2_cond_W_down, L2_cond_b_down)
    x = x + _L3_cond_ref(x, cond_8, L3_cond_skill_gate, L3_cond_skill_up, L3_cond_skill_down, L3_cond_shared_gate, L3_cond_shared_up, L3_cond_shared_down)
    return x

_drawn_inputs = setup_inputs


def setup_inputs(seed=0):
    import zlib

    import numpy as np

    out = dict(_drawn_inputs(seed))
    spreads = {'L2_cond_b_up': (0.0, 0.8), 'L2_cond_b_gate': (0.0, 0.8), 'L2_cond_b_down': (0.0, 0.1)}
    factors = {'L1_cond_b_base': 5.613}
    for name, (base, spread) in spreads.items():
        noise = np.random.default_rng([zlib.crc32(name.encode()), seed]).standard_normal(out[name].shape)
        drawn = base * np.exp(spread * noise) if base else spread * noise
        out[name] = jnp.asarray(drawn.astype(out[name].dtype))
    for name, factor in factors.items():
        out[name] = (out[name] * factor).astype(out[name].dtype)
    return out
```

```python
from contextlib import ExitStack

import concourse.bass as bass
from concourse import mybir

ALU = mybir.AluOpType
ACT = mybir.ActivationFunctionType
AX = mybir.AxisListType
F32 = mybir.dt.float32
F32R = mybir.dt.float32r
U32 = mybir.dt.uint32

P = 128
B, T, D = 4, 512, 256
KD = D // P
G = 8
H2 = 512
H3 = 1024
TOP_K = 2
W_SCALE = 1.0 / 12
LORA_SCALE = 32.0 / 16
RANK = 16

LIN0 = KD * P
DOWN0 = 2 * KD * P
UNIT = DOWN0 + D
CHUNK = 2
U2 = H2 // P
U3 = H3 // P
C2, C3 = U2 // CHUNK, U3 // CHUNK
RAW = 5
RING = 5
LAG = 2
HID = 4

STREAM = (
    [("shared", i) for i in range(U3)] + [("expert", i) for i in range(U3)]
    + [("layer2", i) for i in range(U2)] + [("expert", U3 + i) for i in range(U3)]
)
LAST_STREAM = [s for s in STREAM if s[0] != "layer2"]
SLOTS = len(STREAM)
STREAMED = U3 + U2 + U3
CHUNKS = STREAMED // CHUNK
assert STREAMED % RING == 0 and CHUNKS % RAW == 0 and SLOTS % HID == 0

AT_EFF, AT_L0, AT_L1 = 3, 6, 10
AT_X0 = 2
AT_L2_END = U3 + U3 + U2 + LAG

C_A, C_B = 0, D
C_W = C_B + D
C_MASK = C_W + KD * D
C_BIAS0 = C_MASK + KD * D
C_BIAS1 = C_BIAS0 + KD
CONSTS = C_BIAS1 + KD
TAB = G + 1
BIAS2 = 2 * U2 + KD


def build(nc, tab, x, w0, consts, w2, bias2, w3, out):
    with ExitStack() as ctx:
        def sb(name, shape, dt=F32):
            return ctx.enter_context(nc.sbuf_tensor(name, shape, dt))

        def bank(name):
            return ctx.enter_context(nc.psum_tensor(name, [P, T], F32))

        def sem(name):
            return ctx.enter_context(nc.semaphore(name))

        tab_sb = sb("tab_sb", [P, B, TAB])
        cur = sb("cur", [P, TAB])
        ranked = sb("ranked", [P, B, G])
        expert_ids = sb("expert_ids", [P, B * G], U32)
        neg_max = sb("neg_max", [P, B])
        exps = sb("exps", [P, B, G])
        exp_sum = sb("exp_sum", [P, B])
        inv_sum = sb("inv_sum", [P, B])
        top_p = sb("top_p", [P, TOP_K, B])
        top_sum = sb("top_sum", [P, B])
        inv_top = sb("inv_top", [P, B])
        top_w = sb("top_w", [P, TOP_K, B])
        top_ws = sb("top_ws", [P, TOP_K, B])
        mix = sb("mix", [P, B, TOP_K])
        cur_mix = sb("cur_mix", [P, TOP_K])

        const_sb = sb("const_sb", [P, CONSTS])
        w0_raw = sb("w0_raw", [P, G, KD * D])
        w0_sum = sb("w0_sum", [P, KD * D])
        w0_h, w0_l = sb("w0_h", [P, KD, D], F32R), sb("w0_l", [P, KD, D], F32R)
        a_h, a_l = sb("a_h", [P, D], F32R), sb("a_l", [P, D], F32R)
        b_f = sb("b_f", [P, D])
        b_h, b_l = sb("b_h", [P, D], F32R), sb("b_l", [P, D], F32R)
        w1_f = sb("w1_f", [P, KD * D])
        w1_h, w1_l = sb("w1_h", [P, KD, D], F32R), sb("w1_l", [P, KD, D], F32R)
        bias2_sb = sb("bias2_sb", [P, BIAS2])

        x_f = sb("x_f", [P, KD, T])
        xf_h, xf_l = sb("xf_h", [P, KD, T], F32R), sb("xf_l", [P, KD, T], F32R)
        x_3 = sb("x_3", [P, KD, T])
        x3_h, x3_l = sb("x3_h", [P, KD, T], F32R), sb("x3_l", [P, KD, T], F32R)
        out_sb = sb("out_sb", [P, KD, T])

        raw = sb("raw", [P, RAW, CHUNK * UNIT])
        ring_h, ring_l = sb("ring_h", [P, RING, UNIT], F32R), sb("ring_l", [P, RING, UNIT], F32R)
        shared_h, shared_l = sb("shared_h", [P, U3, UNIT], F32R), sb("shared_l", [P, U3, UNIT], F32R)
        act_out = sb("act_out", [P, 2, T])
        hid_f = sb("hid_f", [P, 2, T])
        hid_h, hid_l = sb("hid_h", [P, HID, T], F32R), sb("hid_l", [P, HID, T], F32R)

        act_ps = [bank(f"act_ps{i}") for i in range(2)]
        lin_ps = [bank(f"lin_ps{i}") for i in range(2)]
        aux_ps = [bank(f"aux_ps{i}") for i in range(KD)]
        out_ps = [bank(f"out_ps{i}") for i in range(KD)]

        tab_loaded, const_loaded = sem("tab_loaded"), sem("const_loaded")
        w0_loaded = [sem(f"w0_loaded{i}") for i in range(G // 2)]
        x_moved = sem("x_moved")
        bias2_loaded = sem("bias2_loaded")
        raw_loaded = [sem(f"raw_loaded{i}") for i in range(RAW)]
        gate_step, exp_done, mix_copied = sem("gate_step"), sem("exp_done"), sem("mix_copied")
        a_split = sem("a_split")
        cur_copied, b_step = sem("cur_copied"), sem("b_step")
        w0_step, w1_step = sem("w0_step"), sem("w1_step")
        eff_done, l0_done, l1_done = sem("eff_done"), sem("l0_done"), sem("l1_done")
        x_updated, x_high, x_split = sem("x_updated"), sem("x_high"), sem("x_split")
        x3_high, x3_split, x3_copied = sem("x3_high"), sem("x3_split"), sem("x3_copied")
        weight_high, weight_split = sem("weight_high"), sem("weight_split")
        act_ready, lin_ready = sem("act_ready"), sem("lin_ready")
        act_done, hid_done = sem("act_done"), sem("hid_done")
        hid_high, hid_split, down_done = sem("hid_high"), sem("hid_split"), sem("down_done")
        out_ready = sem("out_ready")

        def unit_no(b, slot):
            return b * SLOTS + (U2 + slot)

        def split_no(b, q):
            return b * STREAMED + (U2 + U3 + q)

        RING_UNITS = [s for s, (kind, _) in enumerate(STREAM) if kind != "shared"]
        LAST_RING_UNITS = [s for s, (kind, _) in enumerate(LAST_STREAM) if kind != "shared"]

        def ring_pos(q):
            return (U2 + q) % RING

        def chunk_raw(first, b, j):
            return (first + j) % RAW, b * (CHUNKS // RAW) + ((first + j) // RAW + 1)

        LEAD = C2 + C3
        AUX_W = aux_ps[0]

        def product(pe, ps, w_h, w_l, m_h, m_l, first, last):
            nc.tensor.matmul(ps, w_h, m_h, start=first, stop=False)
            nc.tensor.matmul(ps, w_l, m_h, start=False, stop=False)
            return nc.tensor.matmul(ps, w_h, m_l, start=False, stop=last)

        def up_products(pe, n, par, w_h, w_l, m_h, m_l, may_wait):
            if may_wait:
                pe.wait_ge(act_done, n - 1)
            for k in range(KD):
                last = product(pe, act_ps[par][:, :], w_h[:, k * P:(k + 1) * P], w_l[:, k * P:(k + 1) * P],
                               m_h[:, k, :], m_l[:, k, :], k == 0, k == KD - 1)
            last.then_inc(act_ready, 1)
            if may_wait:
                pe.wait_ge(hid_done, n - 1)
            for k in range(KD):
                c = LIN0 + k * P
                last = product(pe, lin_ps[par][:, :], w_h[:, c:c + P], w_l[:, c:c + P],
                               m_h[:, k, :], m_l[:, k, :], k == 0, k == KD - 1)
            last.then_inc(lin_ready, 1)

        def down_products(pe, n, buf, w_h, w_l, banks, first, final):
            pe.wait_ge(hid_split, n + 1)
            for m in range(KD):
                c = DOWN0 + m * P
                last = product(pe, banks[m][:, :], w_h[:, c:c + P], w_l[:, c:c + P],
                               hid_h[:, buf, :], hid_l[:, buf, :], first, final)
            last.then_inc(down_done, 1)

        def effective_products(pe, b):
            pe.wait_ge(b_step, 3 * b + 3)
            for m in range(KD):
                last = product(pe, AUX_W[:, m * D:(m + 1) * D], a_h[:, m * P:(m + 1) * P], a_l[:, m * P:(m + 1) * P],
                               b_h[:, :], b_l[:, :], True, True)
            last.then_inc(eff_done, 1)

        def dense_products(pe, w_h, w_l, done):
            for m in range(KD):
                for k in range(KD):
                    last = product(pe, aux_ps[m][:, :], w_h[:, k, m * P:(m + 1) * P], w_l[:, k, m * P:(m + 1) * P],
                                   xf_h[:, k, :], xf_l[:, k, :], k == 0, k == KD - 1)
            last.then_inc(done, 1)

        def layer0_products(pe, b):
            pe.wait_ge(w0_step, W0_STEPS * b + W0_STEPS)
            pe.wait_ge(x_split, 3 * b + 1)
            pe.wait_ge(w1_step, 3 * b + 1)
            dense_products(pe, w0_h, w0_l, l0_done)

        def layer1_products(pe, b):
            pe.wait_ge(w1_step, 3 * b + 3)
            pe.wait_ge(x_split, 3 * b + 2)
            dense_products(pe, w1_h, w1_l, l1_done)

        def unit_weights(kind, i, q):
            if kind == "shared":
                return shared_h[:, i, :], shared_l[:, i, :]
            return ring_h[:, ring_pos(q), :], ring_l[:, ring_pos(q), :]

        def split_places(first, b, j, u, kind, i, q):
            buf, times = chunk_raw(first, b, j)
            h, l = unit_weights(kind, i, q)
            return raw[:, buf, u * UNIT:(u + 1) * UNIT], h, l, raw_loaded[buf], times

        def split_high(act, no, places, freed):
            src, h, _, loaded, times = places
            act.wait_ge(loaded, 16 * times)
            if freed is not None:
                act.wait_ge(down_done, freed)
            nc.scalar.activation(h, src, ACT.Copy).then_inc(weight_high, 1)

        def split_low(dve, no, places):
            src, h, l, _, _ = places
            dve.wait_ge(weight_high, no + 1)
            nc.vector.tensor_tensor(l, src, h.bitcast(F32), ALU.subtract).then_inc(weight_split, 1)

        def ring_job(b, q, streamed):
            slot = streamed[q]
            if q < RING:
                freed = unit_no(b, 0)
            else:
                freed = unit_no(b, streamed[q - RING]) + 1
            return split_no(b, q), split_places(LEAD, b, q // CHUNK, q % CHUNK, "ring", 0, q), freed

        def unit_activation(act, n, par, kind, i, may_wait):
            act.wait_ge(act_ready, n + 1)
            if may_wait:
                act.wait_ge(hid_done, n - 1)
            if kind == "layer2":
                nc.scalar.activation(act_out[:, par, :], act_ps[par][:, :], ACT.Silu,
                                     bias=bias2_sb[:, i:i + 1]).then_inc(act_done, 1)
            else:
                nc.scalar.activation(act_out[:, par, :], act_ps[par][:, :],
                                     ACT.Gelu_apprx_tanh).then_inc(act_done, 1)

        def front_high(act, b, step, lead=False):
            if step == 0:
                act.wait_ge(x_moved, 16 * (1 + KD) * b + 16 - (0 if lead else 16 * KD))
            else:
                act.wait_ge(x_updated, 3 * b + step)
            nc.scalar.activation(xf_h[:, :, :], x_f[:, :, :], ACT.Copy).then_inc(x_high, 1)

        def enter_layer3(act, b):
            act.wait_ge(x_updated, 3 * b + 3)
            act.wait_ge(lin_ready, unit_no(b, 0))
            nc.scalar.activation(x3_h[:, :, :], x_f[:, :, :], ACT.Copy).then_inc(x3_high, 1)

        def unit_hidden(dve, n, par, buf, kind, i, may_wait):
            dve.wait_ge(act_done, n + 1)
            dve.wait_ge(lin_ready, n + 1)
            if kind == "shared":
                ins = nc.vector.tensor_tensor(hid_f[:, par, :], act_out[:, par, :], lin_ps[par][:, :], ALU.mult)
            elif kind == "expert":
                e = i // U3
                ins = nc.vector.scalar_tensor_tensor(
                    out=hid_f[:, par, :], in0=act_out[:, par, :], scalar=cur_mix[:, e:e + 1],
                    in1=lin_ps[par][:, :], op0=ALU.mult, op1=ALU.mult)
            else:
                ins = nc.vector.scalar_tensor_tensor(
                    out=hid_f[:, par, :], in0=lin_ps[par][:, :], scalar=bias2_sb[:, U2 + i:U2 + i + 1],
                    in1=act_out[:, par, :], op0=ALU.add, op1=ALU.mult)
            ins.then_inc(hid_done, 1)
            dve.wait_ge(hid_done, n + 1)
            if may_wait:
                dve.wait_ge(down_done, n - (HID - 1))
            nc.vector.tensor_copy(hid_h[:, buf, :], hid_f[:, par, :]).then_inc(hid_high, 1)
            dve.wait_ge(hid_high, n + 1)
            nc.vector.tensor_tensor(hid_l[:, buf, :], hid_f[:, par, :], hid_h[:, buf, :].bitcast(F32),
                                    ALU.subtract).then_inc(hid_split, 1)

        def front_low(dve, b, step):
            dve.wait_ge(x_high, 3 * b + step + 1)
            nc.vector.tensor_tensor(xf_l[:, :, :], x_f[:, :, :], xf_h[:, :, :].bitcast(F32),
                                    ALU.subtract).then_inc(x_split, 1)

        def add_to_x(bias):
            for m in range(KD):
                last = nc.vector.scalar_tensor_tensor(
                    out=x_f[:, m, :], in0=aux_ps[m][:, :], scalar=bias[:, m:m + 1], in1=x_f[:, m, :],
                    op0=ALU.add, op1=ALU.add)
            last.then_inc(x_updated, 1)

        def after_layer0(dve, b):
            dve.wait_ge(l0_done, b + 1)
            add_to_x(const_sb[:, C_BIAS0:C_BIAS0 + KD])

        def after_layer1(dve, b):
            dve.wait_ge(l1_done, b + 1)
            add_to_x(const_sb[:, C_BIAS1:C_BIAS1 + KD])

        def after_layer2(dve, b, used):
            dve.wait_ge(down_done, used)
            add_to_x(bias2_sb[:, 2 * U2:2 * U2 + KD])

        def take_columns(dve, b):
            src = tab_sb[:, b, :] if isinstance(b, int) else tab_sb[:, bass.ds(b, 1), :]
            nc.vector.tensor_copy(cur[:, :], src).then_inc(cur_copied, 1)

        def scale_b(dve, b):
            dve.wait_ge(cur_copied, b + 1)
            nc.vector.tensor_scalar(b_f[:, :], const_sb[:, C_B:C_B + D], cur[:, G:G + 1], LORA_SCALE,
                                    ALU.mult, ALU.mult).then_inc(b_step, 1)
            dve.wait_ge(b_step, 3 * b + 1)
            nc.vector.tensor_copy(b_h[:, :], b_f[:, :]).then_inc(b_step, 1)
            dve.wait_ge(b_step, 3 * b + 2)
            nc.vector.tensor_tensor(b_l[:, :], b_f[:, :], b_h[:, :].bitcast(F32), ALU.subtract).then_inc(b_step, 1)

        W0_STEPS = G + 3

        def w0_steps(dve, b, steps):
            for s in steps:
                if s > 0:
                    dve.wait_ge(w0_step, W0_STEPS * b + s)
                if s == 0:
                    ins = nc.vector.tensor_scalar(w0_sum[:, :], w0_raw[:, 0, :], cur[:, 0:1], None, ALU.mult)
                elif s < G:
                    ins = nc.vector.scalar_tensor_tensor(
                        out=w0_sum[:, :], in0=w0_raw[:, s, :], scalar=cur[:, s:s + 1], in1=w0_sum[:, :],
                        op0=ALU.mult, op1=ALU.add)
                elif s == G:
                    ins = nc.vector.tensor_tensor(w0_sum[:, :], w0_sum[:, :],
                                                  const_sb[:, C_MASK:C_MASK + KD * D], ALU.mult)
                elif s == G + 1:
                    ins = nc.vector.tensor_copy(w0_h.rearrange("p k o -> p (k o)"), w0_sum[:, :])
                else:
                    ins = nc.vector.tensor_tensor(w0_l.rearrange("p k o -> p (k o)"), w0_sum[:, :],
                                                  w0_h.rearrange("p k o -> p (k o)").bitcast(F32), ALU.subtract)
                ins.then_inc(w0_step, 1)

        def finish_w1(dve, b):
            dve.wait_ge(eff_done, b + 1)
            nc.vector.tensor_tensor(w1_f[:, :], AUX_W[:, :], const_sb[:, C_W:C_W + KD * D], ALU.add)\
                .then_inc(w1_step, 1)
            dve.wait_ge(w1_step, 3 * b + 1)
            nc.vector.tensor_copy(w1_h.rearrange("p k o -> p (k o)"), w1_f[:, :]).then_inc(w1_step, 1)
            dve.wait_ge(w1_step, 3 * b + 2)
            nc.vector.tensor_tensor(w1_l.rearrange("p k o -> p (k o)"), w1_f[:, :],
                                    w1_h.rearrange("p k o -> p (k o)").bitcast(F32), ALU.subtract)\
                .then_inc(w1_step, 1)

        def split_layer3_input(dve, b):
            dve.wait_ge(x3_high, b + 1)
            nc.vector.tensor_tensor(x3_l[:, :, :], x_f[:, :, :], x3_h[:, :, :].bitcast(F32),
                                    ALU.subtract).then_inc(x3_split, 1)

        def finish_batch(dve, used):
            dve.wait_ge(down_done, used)
            for m in range(KD):
                nc.vector.tensor_tensor(out_sb[:, m, :], out_ps[m][:, :], x_3[:, m, :], ALU.add)\
                    .then_inc(out_ready, 1)

        block = ctx.enter_context(nc.Block())

        @block.sync
        def _(sp):
            sp.dma_start(tab_sb[:, :, :], tab).then_inc(tab_loaded, 16)
            sp.dma_start(const_sb[:, :], consts).then_inc(const_loaded, 16)
            for i in range(G // 2):
                sp.dma_start(w0_raw[:, 2 * i:2 * i + 2, :], w0[:, 2 * i:2 * i + 2, :]).then_inc(w0_loaded[i], 16)
            sp.wait_ge(gate_step, 2 * B)

            def load_chunk(first, b, j, src, wait):
                buf, _ = chunk_raw(first, b, j)
                if wait:
                    sp.wait_ge(weight_split, b * STREAMED + CHUNK * (first + j - RAW + 1))
                sp.dma_start(raw[:, buf, :], src).then_inc(raw_loaded[buf], 16)

            def load_layer2(first, b, j0, of):
                e2 = sp.value_load(expert_ids[0:1, bass.ds(of * G, 1)], min_val=0, max_val=G - 1)
                if first:
                    sp.wait_ge(x_updated, 3 * of)
                sp.dma_start(bias2_sb[:, :], bias2[bass.ds(e2, 1), :, :]).then_inc(bias2_loaded, 16)
                for c in range(C2):
                    load_chunk(first, b, j0 + c, w2[bass.ds(e2 * C2 + c, 1), :, :], first > 0)

            load_layer2(0, 0, 0, 0)
            for c in range(C3):
                j = C2 + c
                load_chunk(0, 0, j, w3[G * C3 + c, :, :], j >= RAW)

            def load_pass(b, last):
                j = 0
                for e in range(TOP_K):
                    e3 = sp.value_load(expert_ids[0:1, bass.ds(b * G + e, 1)], min_val=0, max_val=G - 1)
                    for c in range(C3):
                        load_chunk(LEAD, b, j, w3[bass.ds(e3 * C3 + c, 1), :, :], True)
                        j += 1
                    if e == 0 and not last:
                        load_layer2(LEAD, b, j, b + 1)
                        j += C2

            with sp.Fori(0, B - 1) as b:
                load_pass(b, False)
            load_pass(B - 1, True)

        @block.tensor
        def _(pe):
            pe.wait_ge(a_split, 2)
            effective_products(pe, 0)
            layer0_products(pe, 0)
            layer1_products(pe, 0)
            pe.wait_ge(x_split, 3)
            for n in range(U2 + LAG):
                if n < U2:
                    pe.wait_ge(weight_split, n + 1)
                    w = unit_weights("layer2", n, n - U2)
                    up_products(pe, n, n % 2, *w, xf_h, xf_l, n >= 2)
                if n >= LAG:
                    d = n - LAG
                    w = unit_weights("layer2", d, d - U2)
                    down_products(pe, d, d % HID, *w, aux_ps, d == 0, d == U2 - 1)

            def one_pass(b, stream):
                streamed = [s for s, (kind, _) in enumerate(stream) if kind != "shared"]
                for s in range(len(stream) + LAG):
                    if stream is STREAM:
                        if s == AT_EFF:
                            effective_products(pe, b + 1)
                        if s == AT_L0:
                            layer0_products(pe, b + 1)
                        if s == AT_L1:
                            layer1_products(pe, b + 1)
                    if s < len(stream):
                        kind, i = stream[s]
                        q = streamed.index(s) if kind != "shared" else 0
                        if s == 0:
                            pe.wait_ge(x3_split, b + 1)
                            pe.wait_ge(weight_split, split_no(0, 0))
                        if kind == "layer2" and i == 0:
                            pe.wait_ge(x_split, 3 * (b + 1) + 3)
                        if kind != "shared":
                            pe.wait_ge(weight_split, split_no(b, q) + 1)
                        front = kind == "layer2"
                        up_products(pe, unit_no(b, s), s % 2, *unit_weights(kind, i, q),
                                    xf_h if front else x3_h, xf_l if front else x3_l, True)
                    if s >= LAG:
                        d = s - LAG
                        kind, i = stream[d]
                        q = streamed.index(d) if kind != "shared" else 0
                        if d == 0:
                            pe.wait_ge(x3_copied, b + 1)
                        if kind == "layer2":
                            down_products(pe, unit_no(b, d), (U2 + d) % HID, *unit_weights(kind, i, q),
                                          aux_ps, i == 0, i == U2 - 1)
                        else:
                            down_products(pe, unit_no(b, d), (U2 + d) % HID, *unit_weights(kind, i, q),
                                          out_ps, d == 0, d == len(stream) - 1)

            with pe.Fori(0, B - 1) as b:
                one_pass(b, STREAM)
            one_pass(B - 1, LAST_STREAM)

        GATE_NEG = 2 * B + 1

        @block.scalar
        def _(act):
            act.dma_start(x_f[:, :, :], x[:, 0, :, :]).then_inc(x_moved, 16)
            act.wait_ge(gate_step, GATE_NEG)
            for b in range(B):
                ins = nc.scalar.activation(exps[:, b, :], ranked[:, b, :], ACT.Exp, bias=neg_max[:, b:b + 1],
                                           accum_out=exp_sum[:, b:b + 1])
            ins.then_inc(exp_done, 1)
            front_high(act, 0, 0, lead=True)

            def lead_high(no):
                if no < U2:
                    places = split_places(0, 0, no // CHUNK, no % CHUNK, "layer2", no, no - U2)
                else:
                    places = split_places(0, 0, no // CHUNK, no % CHUNK, "shared", no - U2, 0)
                split_high(act, no, places, None)

            front_high(act, 0, 1)
            lead_high(0)
            lead_high(1)
            front_high(act, 0, 2)
            lead_high(2)
            lead_high(3)
            act.wait_ge(bias2_loaded, 16)
            for n in range(U2):
                unit_activation(act, n, n % 2, "layer2", n, n >= 2)
                lead_high(U2 + 2 * n)
                lead_high(U2 + 2 * n + 1)

            def next_batch(b):
                nc.scalar.activation(x_3[:, :, :], x_f[:, :, :], ACT.Copy).then_inc(x3_copied, 1)

            def load_x(b):
                act.wait_ge(x3_copied, b)
                act.wait_ge(x3_split, b)
                act.dma_start(x_f[:, :, :], x[:, bass.ds(b, 1), :, :]).then_inc(x_moved, 16)

            def store(b):
                for m in range(KD):
                    act.wait_ge(out_ready, KD * b + m + 1)
                    dst = out[:, b, m, :] if isinstance(b, int) else out[:, bass.ds(b, 1), m, :]
                    act.dma_start(dst, out_sb[:, m, :]).then_inc(x_moved, 16)

            enter_layer3(act, 0)
            next_batch(0)

            def one_pass(b, stream):
                streamed = [s for s, (kind, _) in enumerate(stream) if kind != "shared"]
                for s, (kind, i) in enumerate(stream):
                    if stream is STREAM:
                        if s == AT_X0:
                            front_high(act, b + 1, 0)
                        if s == AT_L0 + 1:
                            front_high(act, b + 1, 1)
                        if s == AT_L1 + 1:
                            front_high(act, b + 1, 2)
                    if kind == "layer2" and i == 0:
                        act.wait_ge(bias2_loaded, 16 * (b + 2))
                    unit_activation(act, unit_no(b, s), s % 2, kind, i, True)
                    if s + 2 in streamed:
                        split_high(act, *ring_job(b, streamed.index(s + 2), streamed))

            with act.Fori(0, B - 1) as b:
                load_x(b + 1)
                one_pass(b, STREAM)
                enter_layer3(act, b + 1)
                store(b)
                next_batch(b + 1)
            one_pass(B - 1, LAST_STREAM)
            store(B - 1)
            act.wait_ge(x_moved, 16 * (1 + KD) * B)

        @block.vector
        def _(dve):
            step = 0

            def gate(ins):
                nonlocal step
                ins.then_inc(gate_step, 1)
                step += 1

            dve.wait_ge(tab_loaded, 16)
            for b in range(B):
                gate(nc.vector.max(ranked[:, b, :], tab_sb[:, b, 0:G]))
            dve.wait_ge(gate_step, step)
            for b in range(B):
                gate(nc.vector.max_index(expert_ids[:, b * G:(b + 1) * G], ranked[:, b, :], tab_sb[:, b, 0:G]))
            dve.wait_ge(gate_step, step)
            gate(nc.vector.tensor_scalar(neg_max[:, :], ranked[:, :, 0], -1.0, None, ALU.mult))
            assert step == GATE_NEG
            take_columns(dve, 0)

            dve.wait_ge(exp_done, 1)
            gate(nc.vector.reciprocal(inv_sum[:, :], exp_sum[:, :]))
            dve.wait_ge(gate_step, step)
            for k in range(TOP_K):
                gate(nc.vector.tensor_tensor(top_p[:, k, :], exps[:, :, k], inv_sum[:, :], ALU.mult))
            dve.wait_ge(gate_step, step)
            gate(nc.vector.tensor_tensor(top_sum[:, :], top_p[:, 0, :], top_p[:, 1, :], ALU.add))
            dve.wait_ge(gate_step, step)
            gate(nc.vector.reciprocal(inv_top[:, :], top_sum[:, :]))
            dve.wait_ge(gate_step, step)
            for k in range(TOP_K):
                gate(nc.vector.tensor_tensor(top_w[:, k, :], top_p[:, k, :], inv_top[:, :], ALU.mult))
            dve.wait_ge(gate_step, step)
            gate(nc.vector.tensor_scalar(top_ws[:, :, :], top_w[:, :, :], W_SCALE, None, ALU.mult))
            dve.wait_ge(gate_step, step)
            for k in range(TOP_K):
                gate(nc.vector.scalar_tensor_tensor(
                    out=mix[:, :, k], in0=top_w[:, k, :], scalar=1.0 - W_SCALE, in1=top_ws[:, k, :],
                    op0=ALU.mult, op1=ALU.add))
            mix_steps = step

            dve.wait_ge(const_loaded, 16)
            nc.vector.tensor_copy(a_h[:, :], const_sb[:, C_A:C_A + D]).then_inc(a_split, 1)
            dve.wait_ge(a_split, 1)
            nc.vector.tensor_tensor(a_l[:, :], const_sb[:, C_A:C_A + D], a_h[:, :].bitcast(F32), ALU.subtract)\
                .then_inc(a_split, 1)
            scale_b(dve, 0)
            front_low(dve, 0, 0)
            for i in range(G // 2):
                dve.wait_ge(w0_loaded[i], 16)
                w0_steps(dve, 0, range(2 * i, 2 * i + 2))
                if i == 0:
                    finish_w1(dve, 0)
            w0_steps(dve, 0, range(G, W0_STEPS))
            after_layer0(dve, 0)
            front_low(dve, 0, 1)

            def lead_low(no):
                if no < U2:
                    places = split_places(0, 0, no // CHUNK, no % CHUNK, "layer2", no, no - U2)
                else:
                    places = split_places(0, 0, no // CHUNK, no % CHUNK, "shared", no - U2, 0)
                split_low(dve, no, places)

            lead_low(0)
            lead_low(1)
            after_layer1(dve, 0)
            front_low(dve, 0, 2)
            lead_low(2)
            lead_low(3)
            dve.wait_ge(bias2_loaded, 16)
            for n in range(U2):
                unit_hidden(dve, n, n % 2, n % HID, "layer2", n, False)
                if n < U2 - 1:
                    lead_low(U2 + 2 * n)
                    lead_low(U2 + 2 * n + 1)
            after_layer2(dve, 0, U2)
            split_layer3_input(dve, 0)
            lead_low(U2 + U3 - 2)
            lead_low(U2 + U3 - 1)
            dve.wait_ge(gate_step, mix_steps)

            W0_AT = {0: range(0, 3), 1: range(3, 6), 2: range(6, 9), 3: range(9, W0_STEPS)}

            def one_pass(b, stream):
                streamed = [s for s, (kind, _) in enumerate(stream) if kind != "shared"]
                src = mix[:, b, :] if isinstance(b, int) else mix[:, bass.ds(b, 1), :]
                nc.vector.tensor_copy(cur_mix[:, :], src).then_inc(mix_copied, 1)
                if stream is STREAM:
                    take_columns(dve, b + 1)
                    scale_b(dve, b + 1)
                for s, (kind, i) in enumerate(stream):
                    if stream is STREAM:
                        if s == AT_L0 + 1:
                            after_layer0(dve, b + 1)
                        if s == AT_L1 + 1:
                            after_layer1(dve, b + 1)
                        if s == AT_L2_END:
                            after_layer2(dve, b + 1, unit_no(b, AT_L2_END - LAG))
                    if kind == "layer2" and i == 0:
                        dve.wait_ge(bias2_loaded, 16 * (b + 2))
                    if kind == "expert" and i == 0:
                        dve.wait_ge(mix_copied, b + 1)
                    unit_hidden(dve, unit_no(b, s), s % 2, (U2 + s) % HID, kind, i, True)
                    if stream is STREAM:
                        if s in W0_AT:
                            w0_steps(dve, b + 1, W0_AT[s])
                        if s == AT_X0 + 2:
                            front_low(dve, b + 1, 0)
                        if s == AT_EFF:
                            finish_w1(dve, b + 1)
                        if s == AT_L0 + 1:
                            front_low(dve, b + 1, 1)
                        if s == AT_L1 + 1:
                            front_low(dve, b + 1, 2)
                    if s + 2 in streamed:
                        no, places, _ = ring_job(b, streamed.index(s + 2), streamed)
                        split_low(dve, no, places)

            with dve.Fori(0, B - 1) as b:
                one_pass(b, STREAM)
                split_layer3_input(dve, b + 1)
                finish_batch(dve, unit_no(b, SLOTS))
            one_pass(B - 1, LAST_STREAM)
            dve.wait_ge(x_moved, 16 * (B + KD * (B - 1)))
            finish_batch(dve, unit_no(B - 1, len(LAST_STREAM)))


def kernel(x, cond_8, L0_cond_weight, L0_cond_mask, L0_cond_bias, L1_cond_W_base, L1_cond_b_base, L1_cond_As,
           L1_cond_Bs, L2_cond_W_up, L2_cond_b_up, L2_cond_W_gate, L2_cond_b_gate, L2_cond_W_down, L2_cond_b_down,
           L3_cond_skill_gate, L3_cond_skill_up, L3_cond_skill_down, L3_cond_shared_gate, L3_cond_shared_up,
           L3_cond_shared_down):
    import numpy as np
    import concourse.bacc as bacc
    from concourse.bass_utils import run_bass_kernel_spmd

    def features_first(a):
        a = np.asarray(a)
        a = a.reshape(*a.shape[:-2], a.shape[-2] // P, P, a.shape[-1])
        return np.moveaxis(a, -2, -3)

    def columns(v):
        return features_first(np.asarray(v)[..., None])[..., 0]

    def units(into_act, linear, down):
        e, _, hidden = into_act.shape
        n = hidden // P

        def up(a):
            a = a.reshape(e, KD, P, n, P).transpose(0, 3, 2, 1, 4)
            return a.reshape(e, n, P, KD * P)

        packed = np.concatenate([up(into_act), up(linear), down.reshape(e, n, P, D)], axis=-1)
        packed = packed.reshape(e, n // CHUNK, CHUNK, P, UNIT).transpose(0, 1, 3, 2, 4)
        return packed.reshape(e * n // CHUNK, P, CHUNK * UNIT)

    def swap(a):
        return np.swapaxes(np.asarray(a), -1, -2)

    cond = np.asarray(cond_8)
    tab = np.concatenate([np.broadcast_to(cond[None], (P, B, G)),
                          np.repeat(cond.T, RANK, axis=0)[:, :, None]], axis=-1)
    consts = np.concatenate([
        np.asarray(L1_cond_As).reshape(G * RANK, D),
        np.asarray(L1_cond_Bs).transpose(0, 2, 1).reshape(G * RANK, D),
        features_first(swap(L1_cond_W_base)).reshape(P, KD * D),
        features_first(swap(L0_cond_mask)).reshape(P, KD * D),
        columns(L0_cond_bias), columns(L1_cond_b_base)], axis=1)
    arrays = {
        "tab": tab,
        "x": features_first(swap(x)).transpose(1, 0, 2, 3),
        "w0": features_first(swap(L0_cond_weight)).transpose(1, 0, 2, 3).reshape(P, G, KD * D),
        "consts": consts,
        "w2": units(swap(L2_cond_W_up), swap(L2_cond_W_gate), swap(L2_cond_W_down)),
        "bias2": np.concatenate([columns(L2_cond_b_up), columns(L2_cond_b_gate), columns(L2_cond_b_down)], axis=-1),
        "w3": units(*(np.concatenate([np.asarray(a), np.asarray(s)[None]]) for a, s in (
            (L3_cond_skill_gate, L3_cond_shared_gate), (L3_cond_skill_up, L3_cond_shared_up),
            (L3_cond_skill_down, L3_cond_shared_down)))),
    }
    arrays = {f"{k}_dram": np.ascontiguousarray(v) for k, v in arrays.items()}

    nc = bacc.Bacc("TRN2", target_bir_lowering=False, num_devices=1)
    ins = [nc.dram_tensor(k, v.shape, mybir.dt.from_np(v.dtype), kind="ExternalInput").ap()
           for k, v in arrays.items()]
    out = nc.dram_tensor("out_dram", (P, B, KD, T), F32, kind="ExternalOutput").ap()
    build(nc, *ins, out)
    r = run_bass_kernel_spmd(nc, [arrays], core_ids=[0])
    got = r.results[0]["out_dram"]
    return np.ascontiguousarray(np.asarray(got).transpose(1, 3, 2, 0).reshape(B, T, D))
```

```python
from contextlib import ExitStack

import concourse.bass as bass
from concourse import mybir

ALU = mybir.AluOpType
ACT = mybir.ActivationFunctionType
AX = mybir.AxisListType
F32 = mybir.dt.float32
F32R = mybir.dt.float32r
U32 = mybir.dt.uint32

P = 128
B, T, D = 4, 512, 256
KD = D // P
G = 8
H2 = 512
H3 = 1024
TOP_K = 2
W_SCALE = 1.0 / 12
LORA_SCALE = 32.0 / 16
RANK = 16

LIN0 = KD * P
DOWN0 = 2 * KD * P
UNIT = DOWN0 + D
CHUNK = 2
U2 = H2 // P
U3 = H3 // P
C2, C3 = U2 // CHUNK, U3 // CHUNK
RAW = 5
RING = 5
LAG = 2
HID = 4

STREAM = (
    [("shared", i) for i in range(U3)] + [("expert", i) for i in range(U3 + U3 // 2)]
    + [("layer2", i) for i in range(U2)] + [("expert", i) for i in range(U3 + U3 // 2, 2 * U3)]
)
LAST_STREAM = [s for s in STREAM if s[0] != "layer2"]
SLOTS = len(STREAM)
STREAMED = U3 + U2 + U3
CHUNKS = STREAMED // CHUNK
assert STREAMED % RING == 0 and CHUNKS % RAW == 0 and SLOTS % HID == 0

OWN_X = 5
AT_COPY_X = 0
AT_LOAD_X = 3
AT_X0 = 5
AT_B, AT_EFF, AT_L0, AT_L1 = 2, 7, 9, 13
W0_AT = {1: range(0, 1), 2: range(1, 3), 3: range(3, 5), 4: range(5, 7), 5: range(7, 9), 6: range(9, G + 3)}
AT_L2_END = STREAM.index(("layer2", U2 - 1)) + LAG + 1

C_A, C_B = 0, D
C_W = C_B + D
C_MASK = C_W + KD * D
C_BIAS0 = C_MASK + KD * D
C_BIAS1 = C_BIAS0 + KD
CONSTS = C_BIAS1 + KD
TAB = G + 1
BIAS2 = 2 * U2 + KD


def build(nc, tab, x, w0, consts, w2, bias2, w3, out):
    with ExitStack() as ctx:
        def sb(name, shape, dt=F32):
            return ctx.enter_context(nc.sbuf_tensor(name, shape, dt))

        def bank(name):
            return ctx.enter_context(nc.psum_tensor(name, [P, T], F32))

        def sem(name):
            return ctx.enter_context(nc.semaphore(name))

        tab_sb = sb("tab_sb", [P, B, TAB])
        cur = sb("cur", [P, TAB])
        ranked = sb("ranked", [P, B, G])
        expert_ids = sb("expert_ids", [P, B * G], U32)
        neg_max = sb("neg_max", [P, B])
        exps = sb("exps", [P, B, G])
        exp_sum = sb("exp_sum", [P, B])
        inv_sum = sb("inv_sum", [P, B])
        top_p = sb("top_p", [P, TOP_K, B])
        top_sum = sb("top_sum", [P, B])
        inv_top = sb("inv_top", [P, B])
        top_w = sb("top_w", [P, TOP_K, B])
        top_ws = sb("top_ws", [P, TOP_K, B])
        mix = sb("mix", [P, B, TOP_K])
        cur_mix = sb("cur_mix", [P, TOP_K])

        const_sb = sb("const_sb", [P, CONSTS])
        w0_raw = sb("w0_raw", [P, G, KD * D])
        w0_sum = sb("w0_sum", [P, KD * D])
        w0_h, w0_l = sb("w0_h", [P, KD, D], F32R), sb("w0_l", [P, KD, D], F32R)
        a_h, a_l = sb("a_h", [P, D], F32R), sb("a_l", [P, D], F32R)
        b_h, b_l = sb("b_h", [P, D], F32R), sb("b_l", [P, D], F32R)
        w1_f = sb("w1_f", [P, KD * D])
        b_f = w1_f[:, 0:D]
        w1_h, w1_l = sb("w1_h", [P, KD, D], F32R), sb("w1_l", [P, KD, D], F32R)
        bias2_sb = sb("bias2_sb", [P, BIAS2])

        x_f = sb("x_f", [P, KD, T])
        xf_h, xf_l = sb("xf_h", [P, 2, KD, T], F32R), sb("xf_l", [P, 2, KD, T], F32R)
        x_3 = sb("x_3", [P, KD, T])
        x3_h, x3_l = sb("x3_h", [P, KD, T], F32R), sb("x3_l", [P, KD, T], F32R)
        out_sb = sb("out_sb", [P, KD, T])

        raw = sb("raw", [P, RAW, CHUNK * UNIT])
        ring_h, ring_l = sb("ring_h", [P, RING, UNIT], F32R), sb("ring_l", [P, RING, UNIT], F32R)
        shared_h, shared_l = sb("shared_h", [P, U3, UNIT], F32R), sb("shared_l", [P, U3, UNIT], F32R)
        act_out = sb("act_out", [P, 2, T])
        hid_f = sb("hid_f", [P, 2, T])
        hid_h, hid_l = sb("hid_h", [P, HID, T], F32R), sb("hid_l", [P, HID, T], F32R)

        act_ps = [bank(f"act_ps{i}") for i in range(2)]
        lin_ps = [bank(f"lin_ps{i}") for i in range(2)]
        aux_ps = [bank(f"aux_ps{i}") for i in range(KD)]
        out_ps = [bank(f"out_ps{i}") for i in range(KD)]

        tab_loaded, l1_loaded, mask_loaded = sem("tab_loaded"), sem("l1_loaded"), sem("mask_loaded")
        w0_loaded = [sem(f"w0_loaded{i}") for i in range(G // 2)]
        x_moved = sem("x_moved")
        bias2_loaded = sem("bias2_loaded")
        raw_loaded = [sem(f"raw_loaded{i}") for i in range(RAW)]
        gate_step, exp_done, mix_copied = sem("gate_step"), sem("exp_done"), sem("mix_copied")
        a_high, a_split = sem("a_high"), sem("a_split")
        cur_copied, b_scaled, b_high, b_split = sem("cur_copied"), sem("b_scaled"), sem("b_high"), sem("b_split")
        w0_step = sem("w0_step")
        w1_added, w1_high, w1_split = sem("w1_added"), sem("w1_high"), sem("w1_split")
        eff_done, l0_done, l1_done, l2_half = sem("eff_done"), sem("l0_done"), sem("l1_done"), sem("l2_half")
        x_updated, x_high, x_split = sem("x_updated"), sem("x_high"), sem("x_split")
        x3_high, x3_split, x3_copied = sem("x3_high"), sem("x3_split"), sem("x3_copied")
        weight_high, weight_split = sem("weight_high"), sem("weight_split")
        act_ready, lin_ready = sem("act_ready"), sem("lin_ready")
        act_done, hid_done = sem("act_done"), sem("hid_done")
        hid_high, hid_split, down_done = sem("hid_high"), sem("hid_split"), sem("down_done")
        out_half, out_ready = sem("out_half"), sem("out_ready")

        def unit_no(b, slot):
            return b * SLOTS + (U2 + slot)

        def split_no(b, q):
            return b * STREAMED + (U2 + U3 + q)

        def update_no(b, step, k):
            return b * (3 * KD) + ((step - 1) * KD + k)

        def x_no(b, step, k):
            return b * (4 * KD) + (step * KD + k)

        def ring_pos(q):
            return (U2 + q) % RING

        def chunk_raw(first, b, j):
            return (first + j) % RAW, b * (CHUNKS // RAW) + ((first + j) // RAW + 1)

        LEAD = C2 + C3
        def product(pe, ps, w_h, w_l, m_h, m_l, first, last):
            nc.tensor.matmul(ps, w_h, m_h, start=first, stop=False)
            nc.tensor.matmul(ps, w_l, m_h, start=False, stop=False)
            return nc.tensor.matmul(ps, w_h, m_l, start=False, stop=last)

        def products_by_chunk(pe, targets, x_h, x_l, x_first, dones):
            for k in range(KD):
                pe.wait_ge(x_high, x_first + (k + 1))
                if k < KD - 1:
                    for ps, w_h, w_l in targets:
                        nc.tensor.matmul(ps, w_h(k), x_h[:, k, :], start=k == 0, stop=False)
                        nc.tensor.matmul(ps, w_l(k), x_h[:, k, :], start=False, stop=False)
                    pe.wait_ge(x_split, x_first + (k + 1))
                    for ps, w_h, w_l in targets:
                        nc.tensor.matmul(ps, w_h(k), x_l[:, k, :], start=False, stop=False)
                    continue
                for t, ((ps, w_h, w_l), done) in enumerate(zip(targets, dones)):
                    nc.tensor.matmul(ps, w_h(k), x_h[:, k, :], start=False, stop=False)
                    nc.tensor.matmul(ps, w_l(k), x_h[:, k, :], start=False, stop=False)
                    if t == 0:
                        pe.wait_ge(x_split, x_first + (k + 1))
                    nc.tensor.matmul(ps, w_h(k), x_l[:, k, :], start=False, stop=True).then_inc(done, 1)

        def first_up_products(pe, n, par, w_h, w_l, x_h, x_l, x_first, may_wait):
            if may_wait:
                pe.wait_ge(act_done, n - 1)
                pe.wait_ge(hid_done, n - 1)
            products_by_chunk(pe, [
                (ps[par][:, :], lambda k, c=c: w_h[:, c + k * P:c + k * P + P], lambda k, c=c: w_l[:, c + k * P:c + k * P + P])
                for ps, c in ((act_ps, 0), (lin_ps, LIN0))], x_h, x_l, x_first, (act_ready, lin_ready))

        def up_products(pe, n, par, w_h, w_l, m_h, m_l, may_wait):
            if may_wait:
                pe.wait_ge(act_done, n - 1)
            for k in range(KD):
                last = product(pe, act_ps[par][:, :], w_h[:, k * P:(k + 1) * P], w_l[:, k * P:(k + 1) * P],
                               m_h[:, k, :], m_l[:, k, :], k == 0, k == KD - 1)
            last.then_inc(act_ready, 1)
            if may_wait:
                pe.wait_ge(hid_done, n - 1)
            for k in range(KD):
                c = LIN0 + k * P
                last = product(pe, lin_ps[par][:, :], w_h[:, c:c + P], w_l[:, c:c + P],
                               m_h[:, k, :], m_l[:, k, :], k == 0, k == KD - 1)
            last.then_inc(lin_ready, 1)

        def down_products(pe, n, buf, w_h, w_l, banks, first, final, half):
            pe.wait_ge(hid_split, n + 1)
            for m in range(KD):
                c = DOWN0 + m * P
                last = product(pe, banks[m][:, :], w_h[:, c:c + P], w_l[:, c:c + P],
                               hid_h[:, buf, :], hid_l[:, buf, :], first, final)
                if final and m == 0:
                    last.then_inc(half, 1)
            last.then_inc(down_done, 1)

        def effective_products(pe, b, ps):
            pe.wait_ge(b_split, b + 1)
            for m in range(KD):
                last = product(pe, ps[:, m * D:(m + 1) * D], a_h[:, m * P:(m + 1) * P], a_l[:, m * P:(m + 1) * P],
                               b_h[:, :], b_l[:, :], True, True)
            last.then_inc(eff_done, 1)

        def layer0_products(pe, b, shares_bank):
            pe.wait_ge(x_split, x_no(b, 0, KD))
            if shares_bank:
                pe.wait_ge(w1_added, b + 1)
            pe.wait_ge(w0_step, W0_STEPS * b + W0_STEPS - 1)
            for m in range(KD):
                cols = slice(m * P, (m + 1) * P)
                for k in range(KD):
                    nc.tensor.matmul(aux_ps[m][:, :], w0_h[:, k, cols], xf_h[:, 0, k, :], start=k == 0, stop=False)
                    nc.tensor.matmul(aux_ps[m][:, :], w0_h[:, k, cols], xf_l[:, 0, k, :], start=False, stop=False)
                if m == 0:
                    pe.wait_ge(w0_step, W0_STEPS * b + W0_STEPS)
                for k in range(KD):
                    last = nc.tensor.matmul(aux_ps[m][:, :], w0_l[:, k, cols], xf_h[:, 0, k, :],
                                            start=False, stop=k == KD - 1)
                last.then_inc(l0_done, 1)

        def layer1_products(pe, b):
            pe.wait_ge(w1_split, b + 1)
            pe.wait_ge(x_updated, update_no(b, 1, KD))
            products_by_chunk(pe, [
                (aux_ps[m][:, :], lambda k, m=m: w1_h[:, k, m * P:(m + 1) * P],
                 lambda k, m=m: w1_l[:, k, m * P:(m + 1) * P]) for m in range(KD)],
                xf_h[:, 1], xf_l[:, 1], x_no(b, 1, 0), (l1_done, l1_done))

        def unit_weights(kind, i, q):
            if kind == "shared":
                return shared_h[:, i, :], shared_l[:, i, :]
            return ring_h[:, ring_pos(q), :], ring_l[:, ring_pos(q), :]

        def split_places(first, b, j, u, kind, i, q):
            buf, times = chunk_raw(first, b, j)
            h, l = unit_weights(kind, i, q)
            return raw[:, buf, u * UNIT:(u + 1) * UNIT], h, l, raw_loaded[buf], times

        def split_high(act, no, places, freed):
            src, h, _, loaded, times = places
            act.wait_ge(loaded, 16 * times)
            if freed is not None:
                act.wait_ge(down_done, freed)
            nc.scalar.activation(h, src, ACT.Copy).then_inc(weight_high, 1)

        def split_low(eng, no, places):
            src, h, l, _, _ = places
            eng.wait_ge(weight_high, no + 1)
            eng.tensor_tensor(l, src, h.bitcast(F32), ALU.subtract).then_inc(weight_split, 1)

        def lead_places(no):
            if no < U2:
                return split_places(0, 0, no // CHUNK, no % CHUNK, "layer2", no, no - U2)
            return split_places(0, 0, no // CHUNK, no % CHUNK, "shared", no - U2, 0)

        def ring_job(b, q, streamed):
            slot = streamed[q]
            if q < RING:
                freed = unit_no(b, 0)
            else:
                freed = unit_no(b, streamed[q - RING]) + 1
            return split_no(b, q), split_places(LEAD, b, q // CHUNK, q % CHUNK, "ring", 0, q), freed

        def unit_activation(act, n, par, kind, i, may_wait):
            act.wait_ge(act_ready, n + 1)
            if may_wait:
                act.wait_ge(hid_done, n - 1)
            if kind == "layer2":
                nc.scalar.activation(act_out[:, par, :], act_ps[par][:, :], ACT.Silu,
                                     bias=bias2_sb[:, i:i + 1]).then_inc(act_done, 1)
            else:
                nc.scalar.activation(act_out[:, par, :], act_ps[par][:, :],
                                     ACT.Gelu_apprx_tanh).then_inc(act_done, 1)

        def front_high(act, b, step, lead=False):
            for k in range(KD):
                if step:
                    act.wait_ge(x_updated, update_no(b, step, k) + 1)
                elif lead:
                    act.wait_ge(x_moved, 16)
                elif k == 0:
                    act.wait_ge(x_moved, 16 * (1 + KD) * b + 16 - 16 * KD)
                nc.scalar.activation(xf_h[:, step % 2, k, :], x_f[:, k, :], ACT.Copy).then_inc(x_high, 1)

        def scale_b(act, b):
            act.wait_ge(cur_copied, b + 1)
            nc.scalar.activation(b_f[:, :], const_sb[:, C_B:C_B + D], ACT.Copy, scale=cur[:, G:G + 1])\
                .then_inc(b_scaled, 1)
            act.wait_ge(b_scaled, b + 1)
            nc.scalar.activation(b_h[:, :], b_f[:, :], ACT.Copy).then_inc(b_high, 1)

        def high_w1(act, b):
            act.wait_ge(w1_added, b + 1)
            nc.scalar.activation(w1_h.rearrange("p k o -> p (k o)"), w1_f[:, :], ACT.Copy).then_inc(w1_high, 1)

        def high_x3(act, b):
            nc.scalar.activation(x3_h[:, :, :], x_f[:, :, :], ACT.Copy).then_inc(x3_high, 1)

        def unit_hidden(dve, n, par, buf, kind, i, may_wait):
            dve.wait_ge(act_done, n + 1)
            dve.wait_ge(lin_ready, n + 1)
            if kind == "shared":
                ins = nc.vector.tensor_tensor(hid_f[:, par, :], act_out[:, par, :], lin_ps[par][:, :], ALU.mult)
            elif kind == "expert":
                e = i // U3
                ins = nc.vector.scalar_tensor_tensor(
                    out=hid_f[:, par, :], in0=act_out[:, par, :], scalar=cur_mix[:, e:e + 1],
                    in1=lin_ps[par][:, :], op0=ALU.mult, op1=ALU.mult)
            else:
                ins = nc.vector.scalar_tensor_tensor(
                    out=hid_f[:, par, :], in0=lin_ps[par][:, :], scalar=bias2_sb[:, U2 + i:U2 + i + 1],
                    in1=act_out[:, par, :], op0=ALU.add, op1=ALU.mult)
            ins.then_inc(hid_done, 1)
            dve.wait_ge(hid_done, n + 1)
            if may_wait:
                dve.wait_ge(down_done, n - (HID - 1))
            nc.vector.tensor_copy(hid_h[:, buf, :], hid_f[:, par, :]).then_inc(hid_high, 1)
            dve.wait_ge(hid_high, n + 1)
            nc.vector.tensor_tensor(hid_l[:, buf, :], hid_f[:, par, :], hid_h[:, buf, :].bitcast(F32),
                                    ALU.subtract).then_inc(hid_split, 1)

        def front_low(eng, b, step):
            for k in range(KD):
                eng.wait_ge(x_high, x_no(b, step, k) + 1)
                eng.tensor_tensor(xf_l[:, step % 2, k, :], x_f[:, k, :], xf_h[:, step % 2, k, :].bitcast(F32),
                                        ALU.subtract).then_inc(x_split, 1)

        def add_to_x(m, bias):
            nc.vector.scalar_tensor_tensor(
                out=x_f[:, m, :], in0=aux_ps[m][:, :], scalar=bias[:, m:m + 1], in1=x_f[:, m, :],
                op0=ALU.add, op1=ALU.add).then_inc(x_updated, 1)

        def after_layer0(dve, b):
            for m in range(KD):
                dve.wait_ge(l0_done, KD * b + m + 1)
                add_to_x(m, const_sb[:, C_BIAS0:C_BIAS0 + KD])

        def after_layer1(dve, b):
            for m in range(KD):
                dve.wait_ge(l1_done, KD * b + m + 1)
                add_to_x(m, const_sb[:, C_BIAS1:C_BIAS1 + KD])

        def after_layer2(dve, b, used):
            dve.wait_ge(l2_half, b + 1)
            add_to_x(0, bias2_sb[:, 2 * U2:2 * U2 + KD])
            dve.wait_ge(down_done, used)
            add_to_x(1, bias2_sb[:, 2 * U2:2 * U2 + KD])

        def take_columns(dve, b):
            src = tab_sb[:, b, :] if isinstance(b, int) else tab_sb[:, bass.ds(b, 1), :]
            nc.vector.tensor_copy(cur[:, :], src).then_inc(cur_copied, 1)

        def low_b(eng, b):
            eng.wait_ge(b_high, b + 1)
            eng.tensor_tensor(b_l[:, :], b_f[:, :], b_h[:, :].bitcast(F32), ALU.subtract).then_inc(b_split, 1)

        W0_STEPS = G + 3

        def w0_steps(dve, b, steps):
            for s in steps:
                if s > 0:
                    dve.wait_ge(w0_step, W0_STEPS * b + s)
                if s == 0:
                    ins = nc.vector.tensor_scalar(w0_sum[:, :], w0_raw[:, 0, :], cur[:, 0:1], None, ALU.mult)
                elif s < G:
                    ins = nc.vector.scalar_tensor_tensor(
                        out=w0_sum[:, :], in0=w0_raw[:, s, :], scalar=cur[:, s:s + 1], in1=w0_sum[:, :],
                        op0=ALU.mult, op1=ALU.add)
                elif s == G:
                    ins = nc.vector.tensor_tensor(w0_sum[:, :], w0_sum[:, :],
                                                  const_sb[:, C_MASK:C_MASK + KD * D], ALU.mult)
                elif s == G + 1:
                    ins = nc.vector.tensor_copy(w0_h.rearrange("p k o -> p (k o)"), w0_sum[:, :])
                else:
                    ins = nc.vector.tensor_tensor(w0_l.rearrange("p k o -> p (k o)"), w0_sum[:, :],
                                                  w0_h.rearrange("p k o -> p (k o)").bitcast(F32), ALU.subtract)
                ins.then_inc(w0_step, 1)

        def add_w1(dve, b, ps):
            dve.wait_ge(eff_done, b + 1)
            nc.vector.scalar_tensor_tensor(
                out=w1_f[:, :], in0=ps[:, :], scalar=LORA_SCALE, in1=const_sb[:, C_W:C_W + KD * D],
                op0=ALU.mult, op1=ALU.add).then_inc(w1_added, 1)

        def low_w1(dve, b):
            dve.wait_ge(w1_high, b + 1)
            nc.vector.tensor_tensor(w1_l.rearrange("p k o -> p (k o)"), w1_f[:, :],
                                    w1_h.rearrange("p k o -> p (k o)").bitcast(F32), ALU.subtract)\
                .then_inc(w1_split, 1)

        def low_x3(dve, b):
            dve.wait_ge(x3_high, b + 1)
            nc.vector.tensor_tensor(x3_l[:, :, :], x_f[:, :, :], x3_h[:, :, :].bitcast(F32),
                                    ALU.subtract).then_inc(x3_split, 1)

        def copy_x3(dve):
            nc.vector.tensor_copy(x_3[:, :, :], x_f[:, :, :]).then_inc(x3_copied, 1)

        def finish_batch(dve, b, used):
            for m in range(KD):
                if m == 0:
                    dve.wait_ge(out_half, b + 1)
                else:
                    dve.wait_ge(down_done, used)
                nc.vector.tensor_tensor(out_sb[:, m, :], out_ps[m][:, :], x_3[:, m, :], ALU.add)\
                    .then_inc(out_ready, 1)

        block = ctx.enter_context(nc.Block())

        @block.sync
        def _(sp):
            sp.dma_start(tab_sb[:, :, :], tab).then_inc(tab_loaded, 16)
            for i in range(G // 2):
                sp.dma_start(w0_raw[:, 2 * i:2 * i + 2, :], w0[:, 2 * i:2 * i + 2, :]).then_inc(w0_loaded[i], 16)
                if i == 1:
                    sp.dma_start(const_sb[:, 0:C_MASK], consts[:, 0:C_MASK]).then_inc(l1_loaded, 16)
            sp.dma_start(const_sb[:, C_MASK:], consts[:, C_MASK:]).then_inc(mask_loaded, 16)
            sp.wait_ge(gate_step, 2 * B)

            def load_chunk(first, b, j, src, wait):
                buf, _ = chunk_raw(first, b, j)
                if wait:
                    sp.wait_ge(weight_split, b * STREAMED + CHUNK * (first + j - RAW + 1))
                sp.dma_start(raw[:, buf, :], src).then_inc(raw_loaded[buf], 16)

            def load_layer2(first, b, j0, of):
                e2 = sp.value_load(expert_ids[0:1, bass.ds(of * G, 1)], min_val=0, max_val=G - 1)
                if first:
                    sp.wait_ge(x_updated, update_no(of, 1, 0))
                sp.dma_start(bias2_sb[:, :], bias2[bass.ds(e2, 1), :, :]).then_inc(bias2_loaded, 16)
                for c in range(C2):
                    load_chunk(first, b, j0 + c, w2[bass.ds(e2 * C2 + c, 1), :, :], first > 0)

            load_layer2(0, 0, 0, 0)
            for c in range(C3):
                j = C2 + c
                load_chunk(0, 0, j, w3[G * C3 + c, :, :], j >= RAW)

            L2_AFTER = (1, C3 // 2 - 1)

            def load_pass(b, last):
                j = 0
                for e in range(TOP_K):
                    e3 = sp.value_load(expert_ids[0:1, bass.ds(b * G + e, 1)], min_val=0, max_val=G - 1)
                    for c in range(C3):
                        load_chunk(LEAD, b, j, w3[bass.ds(e3 * C3 + c, 1), :, :], True)
                        j += 1
                        if (e, c) == L2_AFTER and not last:
                            load_layer2(LEAD, b, j, b + 1)
                            j += C2

            with sp.Fori(0, B - 1) as b:
                load_pass(b, False)
            load_pass(B - 1, True)

        @block.tensor
        def _(pe):
            def keep_clock_up(times):
                for _ in range(times):
                    nc.tensor.matmul(out_ps[1][:, 0:D], a_h[:, 0:P], a_h[:, :], start=True, stop=True)

            pe.wait_ge(a_high, 1)
            keep_clock_up(8)
            pe.wait_ge(a_split, 1)
            effective_products(pe, 0, out_ps[0])
            keep_clock_up(16)
            layer0_products(pe, 0, False)
            layer1_products(pe, 0)
            for n in range(U2 + LAG):
                if n < U2:
                    pe.wait_ge(weight_split, n + 1)
                    w = unit_weights("layer2", n, n - U2)
                    if n == 0:
                        first_up_products(pe, n, n % 2, *w, xf_h[:, 0], xf_l[:, 0], x_no(0, 2, 0), False)
                    else:
                        up_products(pe, n, n % 2, *w, xf_h[:, 0], xf_l[:, 0], n >= 2)
                if n >= LAG:
                    d = n - LAG
                    w = unit_weights("layer2", d, d - U2)
                    down_products(pe, d, d % HID, *w, aux_ps, d == 0, d == U2 - 1, l2_half)

            def one_pass(b, stream):
                streamed = [s for s, (kind, _) in enumerate(stream) if kind != "shared"]
                for s in range(len(stream) + LAG):
                    if stream is STREAM:
                        if s == AT_EFF:
                            effective_products(pe, b + 1, aux_ps[0])
                        if s == AT_L0:
                            layer0_products(pe, b + 1, True)
                        if s == AT_L1:
                            layer1_products(pe, b + 1)
                    if s < len(stream):
                        kind, i = stream[s]
                        q = streamed.index(s) if kind != "shared" else 0
                        w = unit_weights(kind, i, q)
                        if s == OWN_X:
                            pe.wait_ge(x3_split, b + 1)
                        if kind == "layer2" and i == 0:
                            pe.wait_ge(x_split, x_no(b + 1, 2, KD))
                        if kind == "shared":
                            pe.wait_ge(weight_split, U2 + i + 1)
                        else:
                            pe.wait_ge(weight_split, split_no(b, q) + 1)
                        if s == 0:
                            first_up_products(pe, unit_no(b, s), s % 2, *w, xf_h[:, 1], xf_l[:, 1],
                                              x_no(b, 3, 0), True)
                        elif kind == "layer2":
                            up_products(pe, unit_no(b, s), s % 2, *w, xf_h[:, 0], xf_l[:, 0], True)
                        elif s < OWN_X:
                            up_products(pe, unit_no(b, s), s % 2, *w, xf_h[:, 1], xf_l[:, 1], True)
                        else:
                            up_products(pe, unit_no(b, s), s % 2, *w, x3_h, x3_l, True)
                    if s >= LAG:
                        d = s - LAG
                        kind, i = stream[d]
                        q = streamed.index(d) if kind != "shared" else 0
                        w = unit_weights(kind, i, q)
                        if d == 0:
                            pe.wait_ge(x3_copied, b + 1)
                        if kind == "layer2":
                            down_products(pe, unit_no(b, d), (U2 + d) % HID, *w, aux_ps, i == 0, i == U2 - 1, l2_half)
                        else:
                            down_products(pe, unit_no(b, d), (U2 + d) % HID, *w, out_ps, d == 0,
                                          d == len(stream) - 1, out_half)

            with pe.Fori(0, B - 1) as b:
                one_pass(b, STREAM)
            one_pass(B - 1, LAST_STREAM)

        GATE_NEG = 2 * B + 1

        @block.gpsimd
        def _(pool):
            front_low(pool, 0, 0)
            pool.wait_ge(a_high, 1)
            pool.tensor_tensor(a_l[:, :], const_sb[:, C_A:C_A + D], a_h[:, :].bitcast(F32), ALU.subtract)\
                .then_inc(a_split, 1)
            low_b(pool, 0)
            for no in range(U2 + U3):
                split_low(pool, no, lead_places(no))

        @block.scalar
        def _(act):
            act.dma_start(x_f[:, :, :], x[:, 0, :, :]).then_inc(x_moved, 16)
            act.wait_ge(gate_step, GATE_NEG)
            for b in range(B):
                ins = nc.scalar.activation(exps[:, b, :], ranked[:, b, :], ACT.Exp, bias=neg_max[:, b:b + 1],
                                           accum_out=exp_sum[:, b:b + 1])
            ins.then_inc(exp_done, 1)
            front_high(act, 0, 0, lead=True)

            def lead_high(*nos):
                for no in nos:
                    split_high(act, no, lead_places(no), None)

            LEAD_BEHIND = [(5, 6), (7, 8), (9,), (10, 11)]
            assert LEAD_BEHIND[-1][-1] == U2 + U3 - 1
            act.wait_ge(l1_loaded, 16)
            nc.scalar.activation(a_h[:, :], const_sb[:, C_A:C_A + D], ACT.Copy).then_inc(a_high, 1)
            scale_b(act, 0)
            lead_high(0)
            high_w1(act, 0)
            lead_high(1)
            front_high(act, 0, 1)
            lead_high(2, 3)
            front_high(act, 0, 2)
            lead_high(4)
            act.wait_ge(bias2_loaded, 16)
            for n in range(U2):
                unit_activation(act, n, n % 2, "layer2", n, n >= 2)
                lead_high(*LEAD_BEHIND[n])
            front_high(act, 0, 3)

            def load_x(b):
                act.wait_ge(x3_copied, b)
                act.wait_ge(x3_split, b)
                act.dma_start(x_f[:, :, :], x[:, bass.ds(b, 1), :, :]).then_inc(x_moved, 16)

            def store(b):
                for m in range(KD):
                    act.wait_ge(out_ready, KD * b + m + 1)
                    dst = out[:, b, m, :] if isinstance(b, int) else out[:, bass.ds(b, 1), m, :]
                    act.dma_start(dst, out_sb[:, m, :]).then_inc(x_moved, 16)

            def one_pass(b, stream):
                streamed = [s for s, (kind, _) in enumerate(stream) if kind != "shared"]
                for s, (kind, i) in enumerate(stream):
                    if kind == "layer2" and i == 0:
                        act.wait_ge(bias2_loaded, 16 * (b + 2))
                    unit_activation(act, unit_no(b, s), s % 2, kind, i, True)
                    if s + 2 in streamed:
                        split_high(act, *ring_job(b, streamed.index(s + 2), streamed))
                    if s == AT_COPY_X:
                        high_x3(act, b)
                    if stream is STREAM:
                        if s == AT_B:
                            scale_b(act, b + 1)
                        if s == AT_LOAD_X:
                            load_x(b + 1)
                        if s == AT_X0:
                            front_high(act, b + 1, 0)
                        if s == AT_EFF + 1:
                            high_w1(act, b + 1)
                        if s == AT_L0 + 1:
                            front_high(act, b + 1, 1)
                        if s == AT_L1 + 1:
                            front_high(act, b + 1, 2)
                        if s == AT_L2_END:
                            front_high(act, b + 1, 3)

            with act.Fori(0, B - 1) as b:
                one_pass(b, STREAM)
                store(b)
            one_pass(B - 1, LAST_STREAM)
            store(B - 1)
            act.wait_ge(x_moved, 16 * (1 + KD) * B)

        @block.vector
        def _(dve):
            step = 0

            def gate(ins):
                nonlocal step
                ins.then_inc(gate_step, 1)
                step += 1

            def weigh_experts():
                nonlocal step
                dve.wait_ge(exp_done, 1)
                gate(nc.vector.reciprocal(inv_sum[:, :], exp_sum[:, :]))
                dve.wait_ge(gate_step, step)
                for k in range(TOP_K):
                    gate(nc.vector.tensor_tensor(top_p[:, k, :], exps[:, :, k], inv_sum[:, :], ALU.mult))
                dve.wait_ge(gate_step, step)
                gate(nc.vector.tensor_tensor(top_sum[:, :], top_p[:, 0, :], top_p[:, 1, :], ALU.add))
                dve.wait_ge(gate_step, step)
                gate(nc.vector.reciprocal(inv_top[:, :], top_sum[:, :]))
                dve.wait_ge(gate_step, step)
                for k in range(TOP_K):
                    gate(nc.vector.tensor_tensor(top_w[:, k, :], top_p[:, k, :], inv_top[:, :], ALU.mult))
                dve.wait_ge(gate_step, step)
                gate(nc.vector.tensor_scalar(top_ws[:, :, :], top_w[:, :, :], W_SCALE, None, ALU.mult))
                dve.wait_ge(gate_step, step)
                for k in range(TOP_K):
                    gate(nc.vector.scalar_tensor_tensor(
                        out=mix[:, :, k], in0=top_w[:, k, :], scalar=1.0 - W_SCALE, in1=top_ws[:, k, :],
                        op0=ALU.mult, op1=ALU.add))

            dve.wait_ge(tab_loaded, 16)
            for b in range(B):
                gate(nc.vector.max(ranked[:, b, :], tab_sb[:, b, 0:G]))
            dve.wait_ge(gate_step, step)
            for b in range(B):
                gate(nc.vector.max_index(expert_ids[:, b * G:(b + 1) * G], ranked[:, b, :], tab_sb[:, b, 0:G]))
            dve.wait_ge(gate_step, step)
            gate(nc.vector.tensor_scalar(neg_max[:, :], ranked[:, :, 0], -1.0, None, ALU.mult))
            assert step == GATE_NEG
            take_columns(dve, 0)


            dve.wait_ge(cur_copied, 1)
            for i in range(G // 2):
                dve.wait_ge(w0_loaded[i], 16)
                w0_steps(dve, 0, range(2 * i, 2 * i + 2))
            dve.wait_ge(mask_loaded, 16)
            w0_steps(dve, 0, range(G, W0_STEPS))
            add_w1(dve, 0, out_ps[0])
            low_w1(dve, 0)
            after_layer0(dve, 0)
            front_low(dve, 0, 1)
            after_layer1(dve, 0)
            front_low(dve, 0, 2)
            weigh_experts()
            dve.wait_ge(bias2_loaded, 16)
            for n in range(U2):
                unit_hidden(dve, n, n % 2, n % HID, "layer2", n, False)
            after_layer2(dve, 0, U2)
            front_low(dve, 0, 3)
            copy_x3(dve)
            dve.wait_ge(gate_step, step)
            dve.wait_ge(weight_split, U2 + U3)

            def one_pass(b, stream):
                streamed = [s for s, (kind, _) in enumerate(stream) if kind != "shared"]
                src = mix[:, b, :] if isinstance(b, int) else mix[:, bass.ds(b, 1), :]
                nc.vector.tensor_copy(cur_mix[:, :], src).then_inc(mix_copied, 1)
                if stream is STREAM:
                    take_columns(dve, b + 1)
                for s, (kind, i) in enumerate(stream):
                    if stream is STREAM:
                        if s == AT_EFF + 1:
                            add_w1(dve, b + 1, aux_ps[0])
                        if s == AT_L0 + 1:
                            after_layer0(dve, b + 1)
                        if s == AT_L1 + 1:
                            after_layer1(dve, b + 1)
                        if s == AT_L2_END:
                            after_layer2(dve, b + 1, unit_no(b, AT_L2_END - LAG))
                    if kind == "layer2" and i == 0:
                        dve.wait_ge(bias2_loaded, 16 * (b + 2))
                    if kind == "expert" and i == 0:
                        dve.wait_ge(mix_copied, b + 1)
                    unit_hidden(dve, unit_no(b, s), s % 2, (U2 + s) % HID, kind, i, True)
                    if s + 2 in streamed:
                        no, places, _ = ring_job(b, streamed.index(s + 2), streamed)
                        split_low(dve, no, places)
                    if s == AT_COPY_X + 1:
                        low_x3(dve, b)
                    if stream is STREAM:
                        if s == 0:
                            dve.wait_ge(cur_copied, b + 2)
                        if s in W0_AT:
                            w0_steps(dve, b + 1, W0_AT[s])
                        if s == AT_B + 1:
                            low_b(dve, b + 1)
                        if s == AT_X0 + 1:
                            front_low(dve, b + 1, 0)
                        if s == AT_EFF + 2:
                            low_w1(dve, b + 1)
                        if s == AT_L0 + 2:
                            front_low(dve, b + 1, 1)
                        if s == AT_L1 + 2:
                            front_low(dve, b + 1, 2)
                        if s == AT_L2_END:
                            front_low(dve, b + 1, 3)

            with dve.Fori(0, B - 1) as b:
                one_pass(b, STREAM)
                finish_batch(dve, b, unit_no(b, SLOTS))
                dve.wait_ge(out_ready, KD * b + KD)
                copy_x3(dve)
            one_pass(B - 1, LAST_STREAM)
            dve.wait_ge(x_moved, 16 * (B + KD * (B - 1)))
            finish_batch(dve, B - 1, unit_no(B - 1, len(LAST_STREAM)))


def kernel(x, cond_8, L0_cond_weight, L0_cond_mask, L0_cond_bias, L1_cond_W_base, L1_cond_b_base, L1_cond_As,
           L1_cond_Bs, L2_cond_W_up, L2_cond_b_up, L2_cond_W_gate, L2_cond_b_gate, L2_cond_W_down, L2_cond_b_down,
           L3_cond_skill_gate, L3_cond_skill_up, L3_cond_skill_down, L3_cond_shared_gate, L3_cond_shared_up,
           L3_cond_shared_down):
    import numpy as np
    import concourse.bacc as bacc
    from concourse.bass_utils import run_bass_kernel_spmd

    def features_first(a):
        a = np.asarray(a)
        a = a.reshape(*a.shape[:-2], a.shape[-2] // P, P, a.shape[-1])
        return np.moveaxis(a, -2, -3)

    def columns(v):
        return features_first(np.asarray(v)[..., None])[..., 0]

    def units(into_act, linear, down):
        e, _, hidden = into_act.shape
        n = hidden // P

        def up(a):
            a = a.reshape(e, KD, P, n, P).transpose(0, 3, 2, 1, 4)
            return a.reshape(e, n, P, KD * P)

        packed = np.concatenate([up(into_act), up(linear), down.reshape(e, n, P, D)], axis=-1)
        packed = packed.reshape(e, n // CHUNK, CHUNK, P, UNIT).transpose(0, 1, 3, 2, 4)
        return packed.reshape(e * n // CHUNK, P, CHUNK * UNIT)

    def swap(a):
        return np.swapaxes(np.asarray(a), -1, -2)

    cond = np.asarray(cond_8)
    tab = np.concatenate([np.broadcast_to(cond[None], (P, B, G)),
                          np.repeat(cond.T, RANK, axis=0)[:, :, None]], axis=-1)
    consts = np.concatenate([
        np.asarray(L1_cond_As).reshape(G * RANK, D),
        np.asarray(L1_cond_Bs).transpose(0, 2, 1).reshape(G * RANK, D),
        features_first(swap(L1_cond_W_base)).reshape(P, KD * D),
        features_first(swap(L0_cond_mask)).reshape(P, KD * D),
        columns(L0_cond_bias), columns(L1_cond_b_base)], axis=1)
    arrays = {
        "tab": tab,
        "x": features_first(swap(x)).transpose(1, 0, 2, 3),
        "w0": features_first(swap(L0_cond_weight)).transpose(1, 0, 2, 3).reshape(P, G, KD * D),
        "consts": consts,
        "w2": units(swap(L2_cond_W_up), swap(L2_cond_W_gate), swap(L2_cond_W_down)),
        "bias2": np.concatenate([columns(L2_cond_b_up), columns(L2_cond_b_gate), columns(L2_cond_b_down)], axis=-1),
        "w3": units(*(np.concatenate([np.asarray(a), np.asarray(s)[None]]) for a, s in (
            (L3_cond_skill_gate, L3_cond_shared_gate), (L3_cond_skill_up, L3_cond_shared_up),
            (L3_cond_skill_down, L3_cond_shared_down)))),
    }
    arrays = {f"{k}_dram": np.ascontiguousarray(v) for k, v in arrays.items()}

    nc = bacc.Bacc("TRN2", target_bir_lowering=False, num_devices=1)
    ins = [nc.dram_tensor(k, v.shape, mybir.dt.from_np(v.dtype), kind="ExternalInput").ap()
           for k, v in arrays.items()]
    out = nc.dram_tensor("out_dram", (P, B, KD, T), F32, kind="ExternalOutput").ap()
    build(nc, *ins, out)
    r = run_bass_kernel_spmd(nc, [arrays], core_ids=[0])
    got = r.results[0]["out_dram"]
    return np.ascontiguousarray(np.asarray(got).transpose(1, 3, 2, 0).reshape(B, T, D))
```

```python
from contextlib import ExitStack

import concourse.bass as bass
from concourse import mybir

ALU = mybir.AluOpType
ACT = mybir.ActivationFunctionType
F32 = mybir.dt.float32
F32R = mybir.dt.float32r
U32 = mybir.dt.uint32

P = 128
B, T, D = 4, 512, 256
KD = D // P
G = 8
H2 = 512
H3 = 1024
TOP_K = 2
W_SCALE = 1.0 / 12
LORA_SCALE = 32.0 / 16
RANK = 16

LIN0 = KD * P
DOWN0 = 2 * KD * P
UNIT = DOWN0 + D
CHUNK = 2
U2 = H2 // P
U3 = H3 // P
C2, C3 = U2 // CHUNK, U3 // CHUNK
RAW = 5
RING = 5
W0_LOADS = ((0, 2), (2, 4), (4, 6), (6, 7), (7, 8))
LAG = 2
HID = 4

STREAM = (
    [("shared", i) for i in range(U3)] + [("expert", i) for i in range(U3 + U3 // 2)]
    + [("layer2", i) for i in range(U2)] + [("expert", i) for i in range(U3 + U3 // 2, 2 * U3)]
)
LAST_STREAM = [s for s in STREAM if s[0] != "layer2"]
SLOTS = len(STREAM)
STREAMED = U3 + U2 + U3
CHUNKS = STREAMED // CHUNK
assert STREAMED % RING == 0 and CHUNKS % RAW == 0 and SLOTS % HID == 0

OWN_X = 5
AT_COPY_X = 0
AT_LOAD_X = 3
AT_X0 = 5
AT_B, AT_EFF, AT_L0, AT_L1 = 2, 7, 9, 13
W0_AT = {1: range(0, 1), 2: range(1, 3), 3: range(3, 5), 4: range(5, 7), 5: range(7, 9), 6: range(9, G + 3)}
AT_L2_END = STREAM.index(("layer2", U2 - 1)) + LAG + 1

C_A, C_B = 0, D
C_MASK = C_B + D
C_BIAS0 = C_MASK + KD * D
C_BIAS1 = C_BIAS0 + KD
C_W = C_BIAS1 + KD
CONSTS = C_W + KD * D
TAB = G + 1
BIAS2 = 2 * U2 + KD


def build(nc, tab, x, w0, consts, w2, bias2, w3, out):
    with ExitStack() as ctx:
        def sb(name, shape, dt=F32):
            return ctx.enter_context(nc.sbuf_tensor(name, shape, dt))

        def bank(name):
            return ctx.enter_context(nc.psum_tensor(name, [P, T], F32))

        def sem(name):
            return ctx.enter_context(nc.semaphore(name))

        tab_sb = sb("tab_sb", [P, B, TAB])
        cur = sb("cur", [P, TAB])
        ranked = sb("ranked", [P, B, G])
        expert_ids = sb("expert_ids", [P, B * G], U32)
        neg_max = sb("neg_max", [P, B])
        exps = sb("exps", [P, B, G])
        exp_sum = sb("exp_sum", [P, B])
        inv_sum = sb("inv_sum", [P, B])
        top_p = sb("top_p", [P, TOP_K, B])
        top_sum = sb("top_sum", [P, B])
        inv_top = sb("inv_top", [P, B])
        top_w = sb("top_w", [P, TOP_K, B])
        top_ws = sb("top_ws", [P, TOP_K, B])
        mix = sb("mix", [P, B, TOP_K])
        cur_mix = sb("cur_mix", [P, TOP_K])

        const_sb = sb("const_sb", [P, CONSTS])
        mask_sb = const_sb[:, C_MASK:C_MASK + KD * D].rearrange("p (k o) -> p k o", k=KD)
        w0_raw = sb("w0_raw", [P, G, KD, D])
        w0_sum = sb("w0_sum", [P, KD, D])
        w0_h, w0_l = sb("w0_h", [P, KD, D], F32R), sb("w0_l", [P, KD, D], F32R)
        a_h, a_l = sb("a_h", [P, D], F32R), sb("a_l", [P, D], F32R)
        b_h, b_l = sb("b_h", [P, D], F32R), sb("b_l", [P, D], F32R)
        w1_f = sb("w1_f", [P, KD * D])
        b_f = w1_f[:, 0:D]
        w1_h, w1_l = sb("w1_h", [P, KD, D], F32R), sb("w1_l", [P, KD, D], F32R)
        bias2_sb = sb("bias2_sb", [P, BIAS2])

        x_f = sb("x_f", [P, KD, T])
        xf_h, xf_l = sb("xf_h", [P, 2, KD, T], F32R), sb("xf_l", [P, 2, KD, T], F32R)
        x_3 = sb("x_3", [P, KD, T])
        x3_h, x3_l = sb("x3_h", [P, KD, T], F32R), sb("x3_l", [P, KD, T], F32R)
        out_sb = sb("out_sb", [P, KD, T])

        raw = sb("raw", [P, RAW, CHUNK * UNIT])
        ring_h, ring_l = sb("ring_h", [P, RING, UNIT], F32R), sb("ring_l", [P, RING, UNIT], F32R)
        shared_h, shared_l = sb("shared_h", [P, U3, UNIT], F32R), sb("shared_l", [P, U3, UNIT], F32R)
        act_out = sb("act_out", [P, 2, T])
        hid_f = sb("hid_f", [P, 2, T])
        hid_h, hid_l = sb("hid_h", [P, HID, T], F32R), sb("hid_l", [P, HID, T], F32R)

        act_ps = [bank(f"act_ps{i}") for i in range(2)]
        lin_ps = [bank(f"lin_ps{i}") for i in range(2)]
        aux_ps = [bank(f"aux_ps{i}") for i in range(KD)]
        out_ps = [bank(f"out_ps{i}") for i in range(KD)]

        tab_loaded, lora_loaded = sem("tab_loaded"), sem("lora_loaded")
        mask_loaded, base_loaded = sem("mask_loaded"), sem("base_loaded")
        w0_loaded = [sem(f"w0_loaded{i}") for i in range(len(W0_LOADS))]
        x_moved = sem("x_moved")
        bias2_loaded = sem("bias2_loaded")
        raw_loaded = [sem(f"raw_loaded{i}") for i in range(RAW)]
        gate_step, exp_done, mix_copied = sem("gate_step"), sem("exp_done"), sem("mix_copied")
        a_high, a_split = sem("a_high"), sem("a_split")
        cur_copied, b_scaled, b_high, b_split = sem("cur_copied"), sem("b_scaled"), sem("b_high"), sem("b_split")
        w0_step = sem("w0_step")
        w1_scaled, w1_added, w1_high, w1_split = sem("w1_scaled"), sem("w1_added"), sem("w1_high"), sem("w1_split")
        eff_done, l0_done, l1_done, l2_half = sem("eff_done"), sem("l0_done"), sem("l1_done"), sem("l2_half")
        x_updated, x_high, x_split = sem("x_updated"), sem("x_high"), sem("x_split")
        x3_high, x3_split, x3_copied = sem("x3_high"), sem("x3_split"), sem("x3_copied")
        weight_high, weight_split = sem("weight_high"), sem("weight_split")
        act_ready, lin_ready = sem("act_ready"), sem("lin_ready")
        act_done, hid_done = sem("act_done"), sem("hid_done")
        hid_high, hid_split, down_done = sem("hid_high"), sem("hid_split"), sem("down_done")
        out_half, out_ready = sem("out_half"), sem("out_ready")

        def unit_no(b, slot):
            return b * SLOTS + (U2 + slot)

        def split_no(b, q):
            return b * STREAMED + (U2 + U3 + q)

        def update_no(b, step, k):
            return b * (3 * KD) + ((step - 1) * KD + k)

        def x_no(b, step, k):
            return b * (4 * KD) + (step * KD + k)

        def ring_pos(q):
            return (U2 + q) % RING

        def chunk_raw(first, b, j):
            return (first + j) % RAW, b * (CHUNKS // RAW) + ((first + j) // RAW + 1)

        LEAD = C2 + C3
        def product(pe, ps, w_h, w_l, m_h, m_l, first, last):
            nc.tensor.matmul(ps, w_h, m_h, start=first, stop=False)
            nc.tensor.matmul(ps, w_l, m_h, start=False, stop=False)
            return nc.tensor.matmul(ps, w_h, m_l, start=False, stop=last)

        def products_by_chunk(pe, targets, x_h, x_l, x_first, dones):
            for k in range(KD):
                pe.wait_ge(x_high, x_first + (k + 1))
                if k < KD - 1:
                    for ps, w_h, w_l in targets:
                        nc.tensor.matmul(ps, w_h(k), x_h[:, k, :], start=k == 0, stop=False)
                        nc.tensor.matmul(ps, w_l(k), x_h[:, k, :], start=False, stop=False)
                    pe.wait_ge(x_split, x_first + (k + 1))
                    for ps, w_h, w_l in targets:
                        nc.tensor.matmul(ps, w_h(k), x_l[:, k, :], start=False, stop=False)
                    continue
                for t, ((ps, w_h, w_l), done) in enumerate(zip(targets, dones)):
                    nc.tensor.matmul(ps, w_h(k), x_h[:, k, :], start=False, stop=False)
                    nc.tensor.matmul(ps, w_l(k), x_h[:, k, :], start=False, stop=False)
                    if t == 0:
                        pe.wait_ge(x_split, x_first + (k + 1))
                    nc.tensor.matmul(ps, w_h(k), x_l[:, k, :], start=False, stop=True).then_inc(done, 1)

        def first_up_products(pe, n, par, w_h, w_l, x_h, x_l, x_first, may_wait):
            if may_wait:
                pe.wait_ge(act_done, n - 1)
                pe.wait_ge(hid_done, n - 1)
            products_by_chunk(pe, [
                (ps[par][:, :], lambda k, c=c: w_h[:, c + k * P:c + k * P + P],
                 lambda k, c=c: w_l[:, c + k * P:c + k * P + P])
                for ps, c in ((act_ps, 0), (lin_ps, LIN0))], x_h, x_l, x_first, (act_ready, lin_ready))

        def up_products(pe, n, par, w_h, w_l, m_h, m_l, may_wait):
            if may_wait:
                pe.wait_ge(act_done, n - 1)
            for k in range(KD):
                last = product(pe, act_ps[par][:, :], w_h[:, k * P:(k + 1) * P], w_l[:, k * P:(k + 1) * P],
                               m_h[:, k, :], m_l[:, k, :], k == 0, k == KD - 1)
            last.then_inc(act_ready, 1)
            if may_wait:
                pe.wait_ge(hid_done, n - 1)
            for k in range(KD):
                c = LIN0 + k * P
                last = product(pe, lin_ps[par][:, :], w_h[:, c:c + P], w_l[:, c:c + P],
                               m_h[:, k, :], m_l[:, k, :], k == 0, k == KD - 1)
            last.then_inc(lin_ready, 1)

        def down_products(pe, n, buf, w_h, w_l, banks, first, final, half):
            pe.wait_ge(hid_split, n + 1)
            for m in range(KD):
                c = DOWN0 + m * P
                last = product(pe, banks[m][:, :], w_h[:, c:c + P], w_l[:, c:c + P],
                               hid_h[:, buf, :], hid_l[:, buf, :], first, final)
                if final and m == 0:
                    last.then_inc(half, 1)
            last.then_inc(down_done, 1)

        def effective_products(pe, b, ps):
            pe.wait_ge(b_split, b + 1)
            for m in range(KD):
                last = product(pe, ps[:, m * D:(m + 1) * D], a_h[:, m * P:(m + 1) * P], a_l[:, m * P:(m + 1) * P],
                               b_h[:, :], b_l[:, :], True, True)
            last.then_inc(eff_done, 1)

        def layer0_products(pe, b, lead=False):
            pe.wait_ge(x_split, x_no(b, 0, KD))
            if not lead:
                pe.wait_ge(w1_added, b + 1)
                pe.wait_ge(w0_step, w0_no(b, W0_STEPS - 1))
            for m in range(KD):
                cols = slice(m * P, (m + 1) * P)
                if lead:
                    pe.wait_ge(w0_step, W0_HIGH[m])
                for k in range(KD):
                    nc.tensor.matmul(aux_ps[m][:, :], w0_h[:, k, cols], xf_h[:, 0, k, :], start=k == 0, stop=False)
                    nc.tensor.matmul(aux_ps[m][:, :], w0_h[:, k, cols], xf_l[:, 0, k, :], start=False, stop=False)
                if lead:
                    pe.wait_ge(w0_step, W0_LOW[m])
                elif m == 0:
                    pe.wait_ge(w0_step, w0_no(b, W0_STEPS))
                for k in range(KD):
                    last = nc.tensor.matmul(aux_ps[m][:, :], w0_l[:, k, cols], xf_h[:, 0, k, :],
                                            start=False, stop=k == KD - 1)
                last.then_inc(l0_done, 1)

        def layer1_products(pe, b, banks):
            pe.wait_ge(w1_split, b + 1)
            if banks is aux_ps:
                pe.wait_ge(x_updated, update_no(b, 1, KD))
            products_by_chunk(pe, [
                (banks[m][:, :], lambda k, m=m: w1_h[:, k, m * P:(m + 1) * P],
                 lambda k, m=m: w1_l[:, k, m * P:(m + 1) * P]) for m in range(KD)],
                xf_h[:, 1], xf_l[:, 1], x_no(b, 1, 0), (l1_done, l1_done))

        def unit_weights(kind, i, q):
            if kind == "shared":
                return shared_h[:, i, :], shared_l[:, i, :]
            return ring_h[:, ring_pos(q), :], ring_l[:, ring_pos(q), :]

        def split_places(first, b, j, u, kind, i, q):
            buf, times = chunk_raw(first, b, j)
            h, l = unit_weights(kind, i, q)
            return raw[:, buf, u * UNIT:(u + 1) * UNIT], h, l, raw_loaded[buf], times

        def split_high(act, no, places, freed):
            src, h, _, loaded, times = places
            act.wait_ge(loaded, 16 * times)
            if freed is not None:
                act.wait_ge(down_done, freed)
            nc.scalar.activation(h, src, ACT.Copy).then_inc(weight_high, 1)

        def split_low(eng, no, places):
            src, h, l, _, _ = places
            eng.wait_ge(weight_high, no + 1)
            eng.tensor_tensor(l, src, h.bitcast(F32), ALU.subtract).then_inc(weight_split, 1)

        def lead_places(no):
            if no < U2:
                return split_places(0, 0, no // CHUNK, no % CHUNK, "layer2", no, no - U2)
            return split_places(0, 0, no // CHUNK, no % CHUNK, "shared", no - U2, 0)

        def ring_job(b, q, streamed):
            slot = streamed[q]
            if q < RING:
                freed = unit_no(b, 0)
            else:
                freed = unit_no(b, streamed[q - RING]) + 1
            return split_no(b, q), split_places(LEAD, b, q // CHUNK, q % CHUNK, "ring", 0, q), freed

        def unit_activation(act, n, par, kind, i, may_wait):
            act.wait_ge(act_ready, n + 1)
            if may_wait:
                act.wait_ge(hid_done, n - 1)
            if kind == "layer2":
                nc.scalar.activation(act_out[:, par, :], act_ps[par][:, :], ACT.Silu,
                                     bias=bias2_sb[:, i:i + 1]).then_inc(act_done, 1)
            else:
                nc.scalar.activation(act_out[:, par, :], act_ps[par][:, :],
                                     ACT.Gelu_apprx_tanh).then_inc(act_done, 1)

        def front_high(act, b, step, lead=False):
            for k in range(KD):
                if step:
                    act.wait_ge(x_updated, update_no(b, step, k) + 1)
                elif lead:
                    act.wait_ge(x_moved, 16)
                elif k == 0:
                    act.wait_ge(x_moved, 16 * (1 + KD) * b + 16 - 16 * KD)
                nc.scalar.activation(xf_h[:, step % 2, k, :], x_f[:, k, :], ACT.Copy).then_inc(x_high, 1)

        def scale_b(act, b):
            act.wait_ge(cur_copied, b + 1)
            nc.scalar.activation(b_f[:, :], const_sb[:, C_B:C_B + D], ACT.Copy, scale=cur[:, G:G + 1])\
                .then_inc(b_scaled, 1)
            act.wait_ge(b_scaled, b + 1)
            nc.scalar.activation(b_h[:, :], b_f[:, :], ACT.Copy).then_inc(b_high, 1)

        def high_w1(act, b):
            act.wait_ge(w1_added, b + 1)
            nc.scalar.activation(w1_h.rearrange("p k o -> p (k o)"), w1_f[:, :], ACT.Copy).then_inc(w1_high, 1)

        def high_x3(act, b):
            nc.scalar.activation(x3_h[:, :, :], x_f[:, :, :], ACT.Copy).then_inc(x3_high, 1)

        def unit_hidden(dve, n, par, buf, kind, i, may_wait):
            dve.wait_ge(act_done, n + 1)
            dve.wait_ge(lin_ready, n + 1)
            if kind == "shared":
                ins = nc.vector.tensor_tensor(hid_f[:, par, :], act_out[:, par, :], lin_ps[par][:, :], ALU.mult)
            elif kind == "expert":
                e = i // U3
                ins = nc.vector.scalar_tensor_tensor(
                    out=hid_f[:, par, :], in0=act_out[:, par, :], scalar=cur_mix[:, e:e + 1],
                    in1=lin_ps[par][:, :], op0=ALU.mult, op1=ALU.mult)
            else:
                ins = nc.vector.scalar_tensor_tensor(
                    out=hid_f[:, par, :], in0=lin_ps[par][:, :], scalar=bias2_sb[:, U2 + i:U2 + i + 1],
                    in1=act_out[:, par, :], op0=ALU.add, op1=ALU.mult)
            ins.then_inc(hid_done, 1)
            dve.wait_ge(hid_done, n + 1)
            if may_wait:
                dve.wait_ge(down_done, n - (HID - 1))
            nc.vector.tensor_copy(hid_h[:, buf, :], hid_f[:, par, :]).then_inc(hid_high, 1)
            dve.wait_ge(hid_high, n + 1)
            nc.vector.tensor_tensor(hid_l[:, buf, :], hid_f[:, par, :], hid_h[:, buf, :].bitcast(F32),
                                    ALU.subtract).then_inc(hid_split, 1)

        def front_low(eng, b, step):
            for k in range(KD):
                eng.wait_ge(x_high, x_no(b, step, k) + 1)
                eng.tensor_tensor(xf_l[:, step % 2, k, :], x_f[:, k, :], xf_h[:, step % 2, k, :].bitcast(F32),
                                        ALU.subtract).then_inc(x_split, 1)

        def add_to_x(m, bias, banks=aux_ps):
            nc.vector.scalar_tensor_tensor(
                out=x_f[:, m, :], in0=banks[m][:, :], scalar=bias[:, m:m + 1], in1=x_f[:, m, :],
                op0=ALU.add, op1=ALU.add).then_inc(x_updated, 1)

        def after_layer0(dve, b):
            for m in range(KD):
                dve.wait_ge(l0_done, KD * b + m + 1)
                add_to_x(m, const_sb[:, C_BIAS0:C_BIAS0 + KD])

        def after_layer1(dve, b, banks):
            for m in range(KD):
                dve.wait_ge(l1_done, KD * b + m + 1)
                add_to_x(m, const_sb[:, C_BIAS1:C_BIAS1 + KD], banks)

        def after_layer2(dve, b, used):
            dve.wait_ge(l2_half, b + 1)
            add_to_x(0, bias2_sb[:, 2 * U2:2 * U2 + KD])
            dve.wait_ge(down_done, used)
            add_to_x(1, bias2_sb[:, 2 * U2:2 * U2 + KD])

        def take_columns(dve, b):
            src = tab_sb[:, b, :] if isinstance(b, int) else tab_sb[:, bass.ds(b, 1), :]
            nc.vector.tensor_copy(cur[:, :], src).then_inc(cur_copied, 1)

        def low_b(eng, b):
            eng.wait_ge(b_high, b + 1)
            eng.tensor_tensor(b_l[:, :], b_f[:, :], b_h[:, :].bitcast(F32), ALU.subtract).then_inc(b_split, 1)

        W0_STEPS = G + 3

        def w0_no(b, step):
            return b * W0_STEPS + (W0_LEAD - W0_STEPS + step)

        def add_group(g, cols):
            c = cur[:, g:g + 1]
            if g == 0:
                return nc.vector.tensor_scalar(w0_sum[:, :, cols], w0_raw[:, g, :, cols], c, None, ALU.mult)
            return nc.vector.scalar_tensor_tensor(
                out=w0_sum[:, :, cols], in0=w0_raw[:, g, :, cols], scalar=c, in1=w0_sum[:, :, cols],
                op0=ALU.mult, op1=ALU.add)

        def apply_mask(cols):
            return nc.vector.tensor_tensor(w0_sum[:, :, cols], w0_sum[:, :, cols], mask_sb[:, :, cols], ALU.mult)

        def high_w0(cols):
            return nc.vector.tensor_copy(w0_h[:, :, cols], w0_sum[:, :, cols])

        def low_w0(cols):
            return nc.vector.tensor_tensor(w0_l[:, :, cols], w0_sum[:, :, cols], w0_h[:, :, cols].bitcast(F32),
                                           ALU.subtract)

        def w0_steps(dve, b, steps):
            cols = slice(0, D)
            for s in steps:
                if s > 0:
                    dve.wait_ge(w0_step, w0_no(b, s))
                if s < G:
                    add_group(s, cols).then_inc(w0_step, 1)
                elif s == G:
                    apply_mask(cols).then_inc(w0_step, 1)
                elif s == G + 1:
                    high_w0(cols).then_inc(w0_step, 1)
                else:
                    low_w0(cols).then_inc(w0_step, 1)

        def w0_lead(dve):
            for i, (g0, g1) in enumerate(W0_LOADS):
                dve.wait_ge(w0_loaded[i], 16)
                for g in range(g0, min(g1, G - 1)):
                    if g > 0:
                        dve.wait_ge(w0_step, g)
                    add_group(g, slice(0, D)).then_inc(w0_step, 1)
            dve.wait_ge(w0_step, G - 1)
            dve.wait_ge(mask_loaded, 16)
            left, right = slice(0, P), slice(P, D)
            add_group(G - 1, left).then_inc(w0_step, 1)
            dve.wait_ge(w0_step, G)
            apply_mask(left).then_inc(w0_step, 1)
            dve.wait_ge(w0_step, G + 1)
            high_w0(left).then_inc(w0_step, 1)
            add_group(G - 1, right).then_inc(w0_step, 1)
            dve.wait_ge(w0_step, G + 2)
            low_w0(left).then_inc(w0_step, 1)
            dve.wait_ge(w0_step, G + 3)
            apply_mask(right).then_inc(w0_step, 1)
            dve.wait_ge(w0_step, G + 5)
            high_w0(right).then_inc(w0_step, 1)
            dve.wait_ge(w0_step, G + 6)
            low_w0(right).then_inc(w0_step, 1)

        W0_HIGH, W0_LOW = (G + 2, G + 6), (G + 4, G + 7)
        W0_LEAD = W0_LOW[-1]

        def add_w1(dve, b, ps):
            dve.wait_ge(eff_done, b + 1)
            nc.vector.scalar_tensor_tensor(
                out=w1_f[:, :], in0=ps[:, :], scalar=LORA_SCALE, in1=const_sb[:, C_W:C_W + KD * D],
                op0=ALU.mult, op1=ALU.add).then_inc(w1_added, 1)

        def scale_w1(act, ps):
            act.wait_ge(eff_done, 1)
            nc.scalar.activation(w1_f[:, :], ps[:, :], ACT.Copy, scale=LORA_SCALE).then_inc(w1_scaled, 1)

        def add_base(pool):
            pool.wait_ge(base_loaded, 16)
            pool.wait_ge(w1_scaled, 1)
            pool.tensor_tensor(w1_f[:, :], w1_f[:, :], const_sb[:, C_W:C_W + KD * D], ALU.add).then_inc(w1_added, 1)

        def low_w1(eng, b):
            eng.wait_ge(w1_high, b + 1)
            eng.tensor_tensor(w1_l.rearrange("p k o -> p (k o)"), w1_f[:, :],
                              w1_h.rearrange("p k o -> p (k o)").bitcast(F32), ALU.subtract).then_inc(w1_split, 1)

        def low_x3(dve, b):
            dve.wait_ge(x3_high, b + 1)
            nc.vector.tensor_tensor(x3_l[:, :, :], x_f[:, :, :], x3_h[:, :, :].bitcast(F32),
                                    ALU.subtract).then_inc(x3_split, 1)

        def copy_x3(dve):
            nc.vector.tensor_copy(x_3[:, :, :], x_f[:, :, :]).then_inc(x3_copied, 1)

        def finish_batch(dve, b, used):
            for m in range(KD):
                if m == 0:
                    dve.wait_ge(out_half, b + 1)
                else:
                    dve.wait_ge(down_done, used)
                nc.vector.tensor_tensor(out_sb[:, m, :], out_ps[m][:, :], x_3[:, m, :], ALU.add)\
                    .then_inc(out_ready, 1)

        block = ctx.enter_context(nc.Block())

        @block.sync
        def _(sp):
            sp.dma_start(tab_sb[:, :, :], tab).then_inc(tab_loaded, 16)
            for i, (g0, g1) in enumerate(W0_LOADS):
                sp.dma_start(w0_raw[:, g0:g1, :], w0[:, g0:g1, :]).then_inc(w0_loaded[i], 16)
                if i == 1:
                    sp.dma_start(const_sb[:, C_A:C_MASK], consts[:, C_A:C_MASK]).then_inc(lora_loaded, 16)
                if i == 2:
                    sp.dma_start(const_sb[:, C_MASK:C_W], consts[:, C_MASK:C_W]).then_inc(mask_loaded, 16)
            sp.dma_start(const_sb[:, C_W:], consts[:, C_W:]).then_inc(base_loaded, 16)
            sp.wait_ge(gate_step, 2 * B)

            def load_chunk(first, b, j, src, wait):
                buf, _ = chunk_raw(first, b, j)
                if wait:
                    sp.wait_ge(weight_split, b * STREAMED + CHUNK * (first + j - RAW + 1))
                sp.dma_start(raw[:, buf, :], src).then_inc(raw_loaded[buf], 16)

            def load_layer2(first, b, j0, of):
                e2 = sp.value_load(expert_ids[0:1, bass.ds(of * G, 1)], min_val=0, max_val=G - 1)
                if first:
                    sp.wait_ge(x_updated, update_no(of, 1, 0))
                sp.dma_start(bias2_sb[:, :], bias2[bass.ds(e2, 1), :, :]).then_inc(bias2_loaded, 16)
                for c in range(C2):
                    load_chunk(first, b, j0 + c, w2[bass.ds(e2 * C2 + c, 1), :, :], first > 0)

            load_layer2(0, 0, 0, 0)
            for c in range(C3):
                j = C2 + c
                load_chunk(0, 0, j, w3[G * C3 + c, :, :], j >= RAW)

            L2_AFTER = (1, C3 // 2 - 1)

            def load_pass(b, last):
                j = 0
                for e in range(TOP_K):
                    e3 = sp.value_load(expert_ids[0:1, bass.ds(b * G + e, 1)], min_val=0, max_val=G - 1)
                    for c in range(C3):
                        load_chunk(LEAD, b, j, w3[bass.ds(e3 * C3 + c, 1), :, :], True)
                        j += 1
                        if (e, c) == L2_AFTER and not last:
                            load_layer2(LEAD, b, j, b + 1)
                            j += C2

            with sp.Fori(0, B - 1) as b:
                load_pass(b, False)
            load_pass(B - 1, True)

        @block.tensor
        def _(pe):
            def keep_clock_up(times):
                for _ in range(times):
                    nc.tensor.matmul(out_ps[1][:, 0:D], xf_h[:, 0, 0, 0:P], xf_h[:, 0, 0, 0:D], start=True, stop=True)

            pe.wait_ge(x_high, 1)
            keep_clock_up(22)
            pe.wait_ge(a_split, 1)
            effective_products(pe, 0, out_ps[0])
            keep_clock_up(20)
            layer0_products(pe, 0, lead=True)
            layer1_products(pe, 0, out_ps)
            for n in range(U2 + LAG):
                if n < U2:
                    pe.wait_ge(weight_split, n + 1)
                    w = unit_weights("layer2", n, n - U2)
                    if n == 0:
                        first_up_products(pe, n, n % 2, *w, xf_h[:, 0], xf_l[:, 0], x_no(0, 2, 0), False)
                    else:
                        up_products(pe, n, n % 2, *w, xf_h[:, 0], xf_l[:, 0], n >= 2)
                if n >= LAG:
                    d = n - LAG
                    w = unit_weights("layer2", d, d - U2)
                    down_products(pe, d, d % HID, *w, aux_ps, d == 0, d == U2 - 1, l2_half)

            def one_pass(b, stream):
                streamed = [s for s, (kind, _) in enumerate(stream) if kind != "shared"]
                for s in range(len(stream) + LAG):
                    if stream is STREAM:
                        if s == AT_EFF:
                            effective_products(pe, b + 1, aux_ps[0])
                        if s == AT_L0:
                            layer0_products(pe, b + 1)
                        if s == AT_L1:
                            layer1_products(pe, b + 1, aux_ps)
                    if s < len(stream):
                        kind, i = stream[s]
                        q = streamed.index(s) if kind != "shared" else 0
                        w = unit_weights(kind, i, q)
                        if s == OWN_X:
                            pe.wait_ge(x3_split, b + 1)
                        if kind == "layer2" and i == 0:
                            pe.wait_ge(x_split, x_no(b + 1, 2, KD))
                        if kind == "shared":
                            pe.wait_ge(weight_split, U2 + i + 1)
                        else:
                            pe.wait_ge(weight_split, split_no(b, q) + 1)
                        if s == 0:
                            first_up_products(pe, unit_no(b, s), s % 2, *w, xf_h[:, 1], xf_l[:, 1],
                                              x_no(b, 3, 0), True)
                        elif kind == "layer2":
                            up_products(pe, unit_no(b, s), s % 2, *w, xf_h[:, 0], xf_l[:, 0], True)
                        elif s < OWN_X:
                            up_products(pe, unit_no(b, s), s % 2, *w, xf_h[:, 1], xf_l[:, 1], True)
                        else:
                            up_products(pe, unit_no(b, s), s % 2, *w, x3_h, x3_l, True)
                    if s >= LAG:
                        d = s - LAG
                        kind, i = stream[d]
                        q = streamed.index(d) if kind != "shared" else 0
                        w = unit_weights(kind, i, q)
                        if d == 0:
                            pe.wait_ge(x3_copied, b + 1)
                        if kind == "layer2":
                            down_products(pe, unit_no(b, d), (U2 + d) % HID, *w, aux_ps, i == 0, i == U2 - 1, l2_half)
                        else:
                            down_products(pe, unit_no(b, d), (U2 + d) % HID, *w, out_ps, d == 0,
                                          d == len(stream) - 1, out_half)

            with pe.Fori(0, B - 1) as b:
                one_pass(b, STREAM)
            one_pass(B - 1, LAST_STREAM)

        GATE_NEG = 2 * B + 1

        @block.gpsimd
        def _(pool):
            front_low(pool, 0, 0)
            pool.wait_ge(a_high, 1)
            pool.tensor_tensor(a_l[:, :], const_sb[:, C_A:C_A + D], a_h[:, :].bitcast(F32), ALU.subtract)\
                .then_inc(a_split, 1)
            low_b(pool, 0)
            add_base(pool)
            low_w1(pool, 0)
            for no in range(U2 + U3):
                split_low(pool, no, lead_places(no))

        @block.scalar
        def _(act):
            act.dma_start(x_f[:, :, :], x[:, 0, :, :]).then_inc(x_moved, 16)
            act.wait_ge(gate_step, GATE_NEG)
            for b in range(B):
                ins = nc.scalar.activation(exps[:, b, :], ranked[:, b, :], ACT.Exp, bias=neg_max[:, b:b + 1],
                                           accum_out=exp_sum[:, b:b + 1])
            ins.then_inc(exp_done, 1)
            front_high(act, 0, 0, lead=True)

            def lead_high(*nos):
                for no in nos:
                    split_high(act, no, lead_places(no), None)

            LEAD_BEHIND = [(5, 6), (7, 8), (9,), (10, 11)]
            assert LEAD_BEHIND[-1][-1] == U2 + U3 - 1
            act.wait_ge(lora_loaded, 16)
            nc.scalar.activation(a_h[:, :], const_sb[:, C_A:C_A + D], ACT.Copy).then_inc(a_high, 1)
            scale_b(act, 0)
            scale_w1(act, out_ps[0])
            high_w1(act, 0)
            front_high(act, 0, 1)
            lead_high(0, 1, 2)
            front_high(act, 0, 2)
            lead_high(3, 4)
            act.wait_ge(bias2_loaded, 16)
            for n in range(U2):
                unit_activation(act, n, n % 2, "layer2", n, n >= 2)
                lead_high(*LEAD_BEHIND[n])
            front_high(act, 0, 3)

            def load_x(b):
                act.wait_ge(x3_copied, b)
                act.wait_ge(x3_split, b)
                act.dma_start(x_f[:, :, :], x[:, bass.ds(b, 1), :, :]).then_inc(x_moved, 16)

            def store(b):
                for m in range(KD):
                    act.wait_ge(out_ready, KD * b + m + 1)
                    dst = out[:, b, m, :] if isinstance(b, int) else out[:, bass.ds(b, 1), m, :]
                    act.dma_start(dst, out_sb[:, m, :]).then_inc(x_moved, 16)

            def one_pass(b, stream):
                streamed = [s for s, (kind, _) in enumerate(stream) if kind != "shared"]
                for s, (kind, i) in enumerate(stream):
                    if kind == "layer2" and i == 0:
                        act.wait_ge(bias2_loaded, 16 * (b + 2))
                    unit_activation(act, unit_no(b, s), s % 2, kind, i, True)
                    if s + 2 in streamed:
                        split_high(act, *ring_job(b, streamed.index(s + 2), streamed))
                    if s == AT_COPY_X:
                        high_x3(act, b)
                    if stream is STREAM:
                        if s == AT_B:
                            scale_b(act, b + 1)
                        if s == AT_LOAD_X:
                            load_x(b + 1)
                        if s == AT_X0:
                            front_high(act, b + 1, 0)
                        if s == AT_EFF + 1:
                            high_w1(act, b + 1)
                        if s == AT_L0 + 1:
                            front_high(act, b + 1, 1)
                        if s == AT_L1 + 1:
                            front_high(act, b + 1, 2)
                        if s == AT_L2_END:
                            front_high(act, b + 1, 3)

            with act.Fori(0, B - 1) as b:
                one_pass(b, STREAM)
                store(b)
            one_pass(B - 1, LAST_STREAM)
            store(B - 1)
            act.wait_ge(x_moved, 16 * (1 + KD) * B)

        @block.vector
        def _(dve):
            step = 0

            def gate(ins):
                nonlocal step
                ins.then_inc(gate_step, 1)
                step += 1

            def weigh_experts():
                nonlocal step
                dve.wait_ge(exp_done, 1)
                gate(nc.vector.reciprocal(inv_sum[:, :], exp_sum[:, :]))
                dve.wait_ge(gate_step, step)
                for k in range(TOP_K):
                    gate(nc.vector.tensor_tensor(top_p[:, k, :], exps[:, :, k], inv_sum[:, :], ALU.mult))
                dve.wait_ge(gate_step, step)
                gate(nc.vector.tensor_tensor(top_sum[:, :], top_p[:, 0, :], top_p[:, 1, :], ALU.add))
                dve.wait_ge(gate_step, step)
                gate(nc.vector.reciprocal(inv_top[:, :], top_sum[:, :]))
                dve.wait_ge(gate_step, step)
                for k in range(TOP_K):
                    gate(nc.vector.tensor_tensor(top_w[:, k, :], top_p[:, k, :], inv_top[:, :], ALU.mult))
                dve.wait_ge(gate_step, step)
                gate(nc.vector.tensor_scalar(top_ws[:, :, :], top_w[:, :, :], W_SCALE, None, ALU.mult))
                dve.wait_ge(gate_step, step)
                for k in range(TOP_K):
                    gate(nc.vector.scalar_tensor_tensor(
                        out=mix[:, :, k], in0=top_w[:, k, :], scalar=1.0 - W_SCALE, in1=top_ws[:, k, :],
                        op0=ALU.mult, op1=ALU.add))

            dve.wait_ge(tab_loaded, 16)
            for b in range(B):
                gate(nc.vector.max(ranked[:, b, :], tab_sb[:, b, 0:G]))
            dve.wait_ge(gate_step, step)
            for b in range(B):
                gate(nc.vector.max_index(expert_ids[:, b * G:(b + 1) * G], ranked[:, b, :], tab_sb[:, b, 0:G]))
            dve.wait_ge(gate_step, step)
            gate(nc.vector.tensor_scalar(neg_max[:, :], ranked[:, :, 0], -1.0, None, ALU.mult))
            assert step == GATE_NEG
            take_columns(dve, 0)

            dve.wait_ge(cur_copied, 1)
            w0_lead(dve)
            after_layer0(dve, 0)
            front_low(dve, 0, 1)
            after_layer1(dve, 0, out_ps)
            front_low(dve, 0, 2)
            weigh_experts()
            dve.wait_ge(bias2_loaded, 16)
            for n in range(U2):
                unit_hidden(dve, n, n % 2, n % HID, "layer2", n, False)
            after_layer2(dve, 0, U2)
            front_low(dve, 0, 3)
            copy_x3(dve)
            dve.wait_ge(gate_step, step)
            dve.wait_ge(weight_split, U2 + U3)

            def one_pass(b, stream):
                streamed = [s for s, (kind, _) in enumerate(stream) if kind != "shared"]
                src = mix[:, b, :] if isinstance(b, int) else mix[:, bass.ds(b, 1), :]
                nc.vector.tensor_copy(cur_mix[:, :], src).then_inc(mix_copied, 1)
                if stream is STREAM:
                    take_columns(dve, b + 1)
                for s, (kind, i) in enumerate(stream):
                    if stream is STREAM:
                        if s == AT_EFF + 1:
                            add_w1(dve, b + 1, aux_ps[0])
                        if s == AT_L0 + 1:
                            after_layer0(dve, b + 1)
                        if s == AT_L1 + 1:
                            after_layer1(dve, b + 1, aux_ps)
                        if s == AT_L2_END:
                            after_layer2(dve, b + 1, unit_no(b, AT_L2_END - LAG))
                    if kind == "layer2" and i == 0:
                        dve.wait_ge(bias2_loaded, 16 * (b + 2))
                    if kind == "expert" and i == 0:
                        dve.wait_ge(mix_copied, b + 1)
                    unit_hidden(dve, unit_no(b, s), s % 2, (U2 + s) % HID, kind, i, True)
                    if s + 2 in streamed:
                        no, places, _ = ring_job(b, streamed.index(s + 2), streamed)
                        split_low(dve, no, places)
                    if s == AT_COPY_X + 1:
                        low_x3(dve, b)
                    if stream is STREAM:
                        if s == 0:
                            dve.wait_ge(cur_copied, b + 2)
                        if s in W0_AT:
                            w0_steps(dve, b + 1, W0_AT[s])
                        if s == AT_B + 1:
                            low_b(dve, b + 1)
                        if s == AT_X0 + 1:
                            front_low(dve, b + 1, 0)
                        if s == AT_EFF + 2:
                            low_w1(dve, b + 1)
                        if s == AT_L0 + 2:
                            front_low(dve, b + 1, 1)
                        if s == AT_L1 + 2:
                            front_low(dve, b + 1, 2)
                        if s == AT_L2_END:
                            front_low(dve, b + 1, 3)

            with dve.Fori(0, B - 1) as b:
                one_pass(b, STREAM)
                finish_batch(dve, b, unit_no(b, SLOTS))
                dve.wait_ge(out_ready, KD * b + KD)
                copy_x3(dve)
            one_pass(B - 1, LAST_STREAM)
            dve.wait_ge(x_moved, 16 * (B + KD * (B - 1)))
            finish_batch(dve, B - 1, unit_no(B - 1, len(LAST_STREAM)))


def kernel(x, cond_8, L0_cond_weight, L0_cond_mask, L0_cond_bias, L1_cond_W_base, L1_cond_b_base, L1_cond_As,
           L1_cond_Bs, L2_cond_W_up, L2_cond_b_up, L2_cond_W_gate, L2_cond_b_gate, L2_cond_W_down, L2_cond_b_down,
           L3_cond_skill_gate, L3_cond_skill_up, L3_cond_skill_down, L3_cond_shared_gate, L3_cond_shared_up,
           L3_cond_shared_down):
    import numpy as np
    import concourse.bacc as bacc
    from concourse.bass_utils import run_bass_kernel_spmd

    def features_first(a):
        a = np.asarray(a)
        a = a.reshape(*a.shape[:-2], a.shape[-2] // P, P, a.shape[-1])
        return np.moveaxis(a, -2, -3)

    def columns(v):
        return features_first(np.asarray(v)[..., None])[..., 0]

    def units(into_act, linear, down):
        e, _, hidden = into_act.shape
        n = hidden // P

        def up(a):
            a = a.reshape(e, KD, P, n, P).transpose(0, 3, 2, 1, 4)
            return a.reshape(e, n, P, KD * P)

        packed = np.concatenate([up(into_act), up(linear), down.reshape(e, n, P, D)], axis=-1)
        packed = packed.reshape(e, n // CHUNK, CHUNK, P, UNIT).transpose(0, 1, 3, 2, 4)
        return packed.reshape(e * n // CHUNK, P, CHUNK * UNIT)

    def swap(a):
        return np.swapaxes(np.asarray(a), -1, -2)

    cond = np.asarray(cond_8)
    tab = np.concatenate([np.broadcast_to(cond[None], (P, B, G)),
                          np.repeat(cond.T, RANK, axis=0)[:, :, None]], axis=-1)
    consts = np.concatenate([
        np.asarray(L1_cond_As).reshape(G * RANK, D),
        np.asarray(L1_cond_Bs).transpose(0, 2, 1).reshape(G * RANK, D),
        features_first(swap(L0_cond_mask)).reshape(P, KD * D),
        columns(L0_cond_bias), columns(L1_cond_b_base),
        features_first(swap(L1_cond_W_base)).reshape(P, KD * D)], axis=1)
    arrays = {
        "tab": tab,
        "x": features_first(swap(x)).transpose(1, 0, 2, 3),
        "w0": features_first(swap(L0_cond_weight)).transpose(1, 0, 2, 3),
        "consts": consts,
        "w2": units(swap(L2_cond_W_up), swap(L2_cond_W_gate), swap(L2_cond_W_down)),
        "bias2": np.concatenate([columns(L2_cond_b_up), columns(L2_cond_b_gate), columns(L2_cond_b_down)], axis=-1),
        "w3": units(*(np.concatenate([np.asarray(a), np.asarray(s)[None]]) for a, s in (
            (L3_cond_skill_gate, L3_cond_shared_gate), (L3_cond_skill_up, L3_cond_shared_up),
            (L3_cond_skill_down, L3_cond_shared_down)))),
    }
    arrays = {f"{k}_dram": np.ascontiguousarray(v) for k, v in arrays.items()}

    nc = bacc.Bacc("TRN2", target_bir_lowering=False, num_devices=1)
    ins = [nc.dram_tensor(k, v.shape, mybir.dt.from_np(v.dtype), kind="ExternalInput").ap()
           for k, v in arrays.items()]
    out = nc.dram_tensor("out_dram", (P, B, KD, T), F32, kind="ExternalOutput").ap()
    build(nc, *ins, out)
    r = run_bass_kernel_spmd(nc, [arrays], core_ids=[0])
    got = r.results[0]["out_dram"]
    return np.ascontiguousarray(np.asarray(got).transpose(1, 3, 2, 0).reshape(B, T, D))
```
